# Optimizing a Trainium2 kernel written in Bass

```python
import numpy as np
import jax
import jax.numpy as jnp

def _softmax(x, axis=-1):
    return jax.nn.softmax(x, axis=axis)

def _gelu(x):
    return jax.nn.gelu(x, approximate=True)

def _silu(x):
    return jax.nn.silu(x)

def _sigmoid(x):
    return jax.nn.sigmoid(x)

def _layernorm(x, axis=-1, eps=1e-05):
    m = jnp.mean(x, axis=axis, keepdims=True)
    v = jnp.var(x, axis=axis, keepdims=True)
    return (x - m) / jnp.sqrt(v + eps)

def _scatter_add(tgt, idx, src, axis=0):
    return tgt.at[idx].add(src)

def _segment_sum(src, seg, n):
    return jax.ops.segment_sum(src, seg, n)
kernel_name = 'mk_adj_ffn_d1_adj_r2_dc02df'

def setup_inputs(seed: int=0):
    np.random.seed(seed)
    _w = jnp.asarray

    def _rec_inputs():
        import jax
        import jax.numpy as jnp
        _gk = jax.random.key(seed)
        x = -0.0005207 + 1.001 * jax.random.normal(jax.random.fold_in(_gk, 1), (8, 1024, 128), jnp.float32)
        _a = jax.random.bernoulli(jax.random.fold_in(_gk, 2), 0.0078125, (8, 1024, 1024))
        _a = jnp.logical_or(_a, jnp.swapaxes(_a, -1, -2))
        _a = jnp.logical_or(_a, jnp.eye(1024, dtype=bool))
        adj = _a.astype(jnp.int32)
        return (x, adj)
    x, adj = _rec_inputs()

    def _L0_gnn_setup():
        import jax, jax.numpy as jnp
        import numpy as np
        BS, N, D, R = (16, 256, 128, 2)
        key = jax.random.key(seed)
        ks = jax.random.split(key, 9)
        s = 1.0 / np.sqrt(D)
        return {'encoded_spans': jax.random.normal(ks[0], (BS, N, D), dtype=jnp.float32), 'w_rel1': jax.random.normal(ks[1], (R, D, D), dtype=jnp.float32) * s, 'w_root1': jax.random.normal(ks[2], (D, D), dtype=jnp.float32) * s, 'b1': jnp.zeros((D,), dtype=jnp.float32), 'w_rel2': jax.random.normal(ks[3], (R, D, D), dtype=jnp.float32) * s, 'w_root2': jax.random.normal(ks[4], (D, D), dtype=jnp.float32) * s, 'b2': jnp.zeros((D,), dtype=jnp.float32), 'aug_adj': jax.random.randint(ks[5], (BS, N, N), 0, 16, dtype=jnp.int64), 'punct_graph': jax.random.randint(ks[6], (BS, N, N), 0, 16, dtype=jnp.int64)}
    _L0_gnn_all = _L0_gnn_setup()
    _L0_gnn_in = {k: v for k, v in _L0_gnn_all.items() if k in ('w_rel1', 'w_root1', 'b1', 'w_rel2', 'w_root2', 'b2')}
    del _L0_gnn_all

    def _L0_ffn_setup():
        import jax, jax.numpy as jnp
        import numpy as np
        B, S, H, F, E, K = (8, 2048, 128, 256, 16, 2)
        EPS = 1e-05
        key = jax.random.key(seed)
        ks = jax.random.split(key, 9)
        sc = 0.02
        return {'x': jax.random.normal(ks[0], (B, S, H), dtype=jnp.float32), 'gate_w': jax.random.normal(ks[1], (H, E), dtype=jnp.float32) * sc, 'gate_b': jnp.zeros((E,), dtype=jnp.float32), 'w1': jax.random.normal(ks[2], (E, H, F), dtype=jnp.float32) * sc, 'b1': jnp.zeros((E, F), dtype=jnp.float32), 'w2': jax.random.normal(ks[3], (E, F, H), dtype=jnp.float32) * sc, 'b2': jnp.zeros((E, H), dtype=jnp.float32), 'gamma': jnp.ones((H,), dtype=jnp.float32), 'beta': jnp.zeros((H,), dtype=jnp.float32)}
    _L0_ffn_all = _L0_ffn_setup()
    _L0_ffn_in = {k: v for k, v in _L0_ffn_all.items() if k in ('gate_w', 'gate_b', 'w1', 'b1', 'w2', 'b2', 'gamma', 'beta')}
    del _L0_ffn_all
    return {'x': x, 'adj': adj, 'L0_gnn_w_rel1': _L0_gnn_in['w_rel1'], 'L0_gnn_w_root1': _L0_gnn_in['w_root1'], 'L0_gnn_b1': _L0_gnn_in['b1'], 'L0_gnn_w_rel2': _L0_gnn_in['w_rel2'], 'L0_gnn_w_root2': _L0_gnn_in['w_root2'], 'L0_gnn_b2': _L0_gnn_in['b2'], 'L0_ffn_gate_w': _L0_ffn_in['gate_w'], 'L0_ffn_gate_b': _L0_ffn_in['gate_b'], 'L0_ffn_w1': _L0_ffn_in['w1'], 'L0_ffn_b1': _L0_ffn_in['b1'], 'L0_ffn_w2': _L0_ffn_in['w2'], 'L0_ffn_b2': _L0_ffn_in['b2'], 'L0_ffn_gamma': _L0_ffn_in['gamma'], 'L0_ffn_beta': _L0_ffn_in['beta']}

def reference(x, adj, L0_gnn_w_rel1, L0_gnn_w_root1, L0_gnn_b1, L0_gnn_w_rel2, L0_gnn_w_root2, L0_gnn_b2, L0_ffn_gate_w, L0_ffn_gate_b, L0_ffn_w1, L0_ffn_b1, L0_ffn_w2, L0_ffn_b2, L0_ffn_gamma, L0_ffn_beta):
    import jax
    import jax.numpy as jnp

    def _L0_gnn_ref(encoded_spans, w_rel1, w_root1, b1, w_rel2, w_root2, b2, aug_adj, punct_graph):
        import jax, jax.numpy as jnp
        import numpy as np
        BS, N, D, R = (16, 256, 128, 2)
        mask_punct = (punct_graph == 1) & (aug_adj != 1)
        mask_aug = aug_adj == 1
        masks = jnp.stack([mask_punct, mask_aug]).astype(encoded_spans.dtype)
        deg = jnp.maximum(masks.sum(axis=2), 1.0)[..., None]

        def conv(x, w_rel, w_root, b):
            out = jnp.einsum('bnd,de->bne', x, w_root) + b
            for r in range(R):
                agg = jnp.einsum('bij,bid->bjd', masks[r], x) / deg[r]
                out = out + jnp.einsum('bjd,de->bje', agg, w_rel[r])
            return out
        h = jax.nn.elu(conv(encoded_spans, w_rel1, w_root1, b1))
        h = jax.nn.elu(conv(h, w_rel2, w_root2, b2))
        return h

    def _L0_ffn_ref(x, gate_w, gate_b, w1, b1, w2, b2, gamma, beta):
        import jax, jax.numpy as jnp
        import numpy as np
        B, S, H, F, E, K = (8, 2048, 128, 256, 16, 2)
        EPS = 1e-05
        gate_logits = x @ gate_w + gate_b
        topk_vals, topk_idx = jax.lax.top_k(gate_logits, K)
        topk_w = jax.nn.softmax(topk_vals, axis=-1)
        h = jax.nn.relu(jnp.einsum('bsh,ehf->bsef', x, w1) + b1)
        expert_out = jnp.einsum('bsef,efh->bseh', h, w2) + b2
        sel = jnp.take_along_axis(expert_out, topk_idx[:, :, :, None], axis=2)
        moe = jnp.sum(topk_w[..., None] * sel, axis=2)
        y = x + moe
        mu = jnp.mean(y, axis=-1, keepdims=True)
        var = jnp.var(y, axis=-1, keepdims=True)
        return (y - mu) / jnp.sqrt(var + EPS) * gamma + beta
    x = x + _L0_gnn_ref(_layernorm(x, axis=-1), L0_gnn_w_rel1, L0_gnn_w_root1, L0_gnn_b1, L0_gnn_w_rel2, L0_gnn_w_root2, L0_gnn_b2, adj, adj)
    x = x + _L0_ffn_ref(_layernorm(x, axis=-1), L0_ffn_gate_w, L0_ffn_gate_b, L0_ffn_w1, L0_ffn_b1, L0_ffn_w2, L0_ffn_b2, L0_ffn_gamma, L0_ffn_beta)
    return x

_drawn_inputs = setup_inputs


def setup_inputs(seed=0):
    import zlib

    import numpy as np

    out = dict(_drawn_inputs(seed))
    spreads = {'L0_gnn_b1': (0.0, 0.1),
     'L0_gnn_b2': (0.0, 0.1),
     'L0_ffn_gate_b': (0.0, 0.283),
     'L0_ffn_b1': (0.0, 0.8),
     'L0_ffn_b2': (0.0, 0.288),
     'L0_ffn_gamma': (1.0, 0.2),
     'L0_ffn_beta': (0.0, 0.1)}
    factors = {'L0_ffn_w1': 4.021, 'L0_ffn_w2': 3.17}
    for name, (base, spread) in spreads.items():
        noise = np.random.default_rng([zlib.crc32(name.encode()), seed]).standard_normal(out[name].shape)
        drawn = base * np.exp(spread * noise) if base else spread * noise
        out[name] = jnp.asarray(drawn.astype(out[name].dtype))
    for name, factor in factors.items():
        out[name] = (out[name] * factor).astype(out[name].dtype)
    return out
```

```python
import concourse.bass as bass
from concourse import mybir
from contextlib import ExitStack


def gnn_moe_kernel(nc, x_d, adj_d, w_rel1_d, w_root1_d, b1g_d, w_rel2_d, w_root2_d, b2g_d,
                   gate_w_d, gate_b_d, w1_d, b1_d, w2_d, b2_d, gamma_d, beta_d, out_d):
    f32, f32r = mybir.dt.float32, mybir.dt.float32r
    bf16, i32, u32 = mybir.dt.bfloat16, mybir.dt.int32, mybir.dt.uint32
    ALU = mybir.AluOpType
    ACT = mybir.ActivationFunctionType
    AX = mybir.AxisListType

    NB, N, H = x_d.shape
    E, _, F = w1_d.shape
    P = 128
    T = N // P
    NT = NB * T
    KSEL = 2
    FH = F // P
    EPS = 1e-5
    NG = 2
    GB = NB // NG
    GT = GB * T
    OCT = 8
    S_T = -(-(GT * KSEL + E - 1) // OCT) * OCT
    NO = S_T // OCT
    SLOTS = S_T * P
    QT = 4
    PAIRS = T // 2
    CQ = GT // QT
    W2C, B1C, B2C = F, F + FH * H, F + FH * H + FH
    PACK = F + FH * H + FH + H
    HALF = N // 2
    AGW = 2 * H + 2

    x_v = x_d.rearrange("b (t p) d -> p (b t) d", p=P)
    out_v = out_d.rearrange("b (t p) d -> p (b t) d", p=P)
    adj_v = adj_d.rearrange("b (i p) j -> b p i j", p=P)
    xs_d = [nc.dram_tensor(f"expert_inputs_{g}", (SLOTS, H), f32).ap() for g in range(NG)]
    y_d = [nc.dram_tensor(f"expert_outputs_{g}", (SLOTS, H), f32).ap() for g in range(NG)]

    ctx = ExitStack()
    with ctx:
        def sb(name, shape, dt=f32):
            return ctx.enter_context(nc.sbuf_tensor(name, shape, dt))

        def pb(name, shape, dt=f32):
            return ctx.enter_context(nc.psum_tensor(name, shape, dt))

        def sem(name):
            return ctx.enter_context(nc.semaphore(name))

        xhat2 = sb("xhat2", [P, NT, H])
        pack = sb("pack", [P, E, PACK])
        mean2 = sb("mean2", [P, NT])
        std2 = sb("std2", [P, NT])
        gates = sb("gates", [P, NT, KSEL])
        pos = sb("pos", [P, NB, KSEL, T], i32)
        emap = sb("emap", [1, NG * S_T + OCT], i32)
        ident = sb("ident", [P, P])
        gamma = sb("gamma", [P, H])
        beta = sb("beta", [P, H])
        adj_st = sb("adj_st", [P, 2, T, HALF], i32)
        mask = sb("mask", [P, T, T, P], f32r)
        xh1 = sb("xh1", [P, T, H])
        yT = xh1[:, :, :].rearrange("p t n -> p (t n)")
        xT = sb("xT", [P, N])
        hT = sb("hT", [P, N])
        h1 = sb("h1", [P, T, H])
        x1b = sb("x1b", [P, T, H])
        zp = [sb(f"zp{c}", [P, T, AGW], f32r) for c in (1, 2)]
        hs = sb("hs", [P, 2, 2, H])
        sm = sb("sm", [P, 2, 2, H])
        vv = sb("vv", [P, 2, 2, H])
        ee = sb("ee", [P, 2, 2, H])
        mm_ = sb("mm_", [P, 2, 2, H])
        dd = sb("dd", [P, 2, 2, 1])
        rd = sb("rd", [P, 2, 2, 1])
        wroot = [sb(f"wroot{c}", [P, H]) for c in (1, 2)]
        wrel = [sb(f"wrel{c}", [P, 2, H]) for c in (1, 2)]
        brow = [sb(f"brow{c}", [P, H]) for c in (1, 2)]
        biasf = sb("biasf", [P, 2, H])
        bhl = sb("bhl", [2, 2, H], f32r)
        ones2 = sb("ones2", [2, P], f32r)
        onez = sb("onez", [P, 2])
        b1rows = sb("b1rows", [E * FH, P])
        bhi = sb("bhi", [2, 2, H], f32r)
        blo = sb("blo", [2, 2, H])
        ones1 = sb("ones1", [2, P])
        zero = sb("zero", [P, 4 * P])
        epsb = sb("epsb", [P, 1])
        st = sb("st", [P, T, 6])
        mv = sb("mv", [P, T, 2])
        lnv = sb("lnv", [P, T])
        rs0 = sb("rs0", [P, T])
        rs1 = sb("rs1", [P, T])
        gate_w = sb("gate_w", [P, E])
        gate_b = sb("gate_b", [P, E])
        logit = sb("logit", [P, T, E])
        top = sb("top", [P, T, 8])
        topi = sb("topi", [P, T, 8], u32)
        sel_e = sb("sel_e", [P, KSEL, T])
        iota_e = sb("iota_e", [P, E])
        iota_s = sb("iota_s", [1, S_T])
        m12 = sb("m12", [P, GB, KSEL, T, E], bf16)
        m1 = sb("m1", [P, T, E], bf16)
        carry = sb("carry", [P, E], bf16)
        carryf = sb("carryf", [P, E])
        msum = sb("msum", [P, E])
        tri = sb("tri", [P, P], bf16)
        onesb = sb("onesb", [P, P], bf16)
        rsel = sb("rsel", [P, KSEL, T, E])
        rank = sb("rank", [P, GB, KSEL, T])
        cnti = sb("cnti", [P, E], i32)
        cntt = sb("cntt", [P, E], i32)
        ntl = sb("ntl", [P, E])
        incl = sb("incl", [P, E])
        base = sb("base", [P, E])
        zer16 = sb("zer16", [P, E])
        past = sb("past", [1, S_T, E], bf16)
        emf = sb("emf", [1, S_T])
        gq = sb("gq", [P, GT])
        gp = sb("gp", [P, GT])
        stage = adj_st[:, :, :, :].rearrange("p a b c -> p (a b c)").bitcast(f32)
        taken = [0]

        def part(n):
            taken[0] += n
            return stage[:, taken[0] - n:taken[0]]

        xs = part(2 * QT * H).rearrange("p (u t d) -> p u t d", u=2, t=QT)
        xsT = part(2 * QT * P).rearrange("p (u n) -> p u n", u=2)
        wc = part(4 * PACK).rearrange("p (r c) -> p r c", r=4)
        ysb = part(2 * QT * H).rearrange("p (u t d) -> p u t d", u=2, t=QT)
        gath = part(2 * QT * KSEL * H).rearrange("p (u n d) -> p u n d", u=2, n=QT * KSEL)
        hA, hB = hs[:, 0, :, :], hs[:, 1, :, :]
        idxg = sb("idxg", [P, 2, KSEL, QT], i32)
        stc = sb("stc", [P, QT, 6])
        mvc = sb("mvc", [P, QT, 2])
        lnc = sb("lnc", [P, QT])
        rc0 = sb("rc0", [P, QT])
        rc1 = sb("rc1", [P, QT])
        yc = xh1[:, 0:QT, :]
        uc = xh1[:, QT:2 * QT, :]
        oc = h1[:, :, :].rearrange("p (u t) d -> p u t d", u=2)

        AG = pb("AG", [P, 4, 512])
        TR = pb("TR", [P, 2, 512])
        ZB = pb("ZB", [P, 512])
        GP = pb("GP", [P, 512])
        YB = [ZB, GP]

        w_in = sem("w_in")
        pack_in = sem("pack_in")
        x0_in, xr_in = sem("x0_in"), sem("xr_in")
        adj_in = [sem(f"adj_in{h}") for h in range(2)]
        xs_zeroed = sem("xs_zeroed")
        scattered = [sem(f"scattered{g}") for g in range(NG)]
        xs_in = [sem(f"xs_in{u}") for u in range(2)]
        y_out = [sem(f"y_out{u}") for u in range(2)]
        gathered = [sem(f"gathered{u}") for u in range(2)]
        o_out = [sem(f"o_out{u}") for u in range(2)]
        pool_const = sem("pool_const")
        pool_idx = sem("pool_idx")
        dve_const = sem("dve_const")
        dve_self = sem("dve_self")
        pe_bias, pe_b1 = sem("pe_bias"), sem("pe_b1")
        act_b1 = sem("act_b1")
        pe_xT, pe_hT, pe_yT = sem("pe_xT"), sem("pe_hT"), sem("pe_yT")
        act_xT, act_hT, act_yT = sem("act_xT"), sem("act_hT"), sem("act_yT")
        pe_z, act_zhi, dve_zlo = sem("pe_z"), sem("act_zhi"), sem("dve_zlo")
        pe_ag, act_aghi, dve_v = sem("pe_ag"), sem("act_aghi"), sem("dve_v")
        act_e, dve_h = sem("act_e"), sem("dve_h")
        dve_mask = sem("dve_mask")
        dve_var, act_ln, act_rs = sem("dve_var"), sem("act_ln"), sem("act_rs")
        dve_xh1, dve_xh2 = sem("dve_xh1"), sem("dve_xh2")
        act_xh2 = sem("act_xh2")
        pe_gate, dve_m1, pe_rank, dve_rank = sem("pe_gate"), sem("dve_m1"), sem("pe_rank"), sem("dve_rank")
        dve_carry = sem("dve_carry")
        pe_cnt, dve_cnt, dve_pos = sem("pe_cnt"), sem("dve_cnt"), sem("dve_pos")
        dve_gd, act_gp = sem("dve_gd"), sem("act_gp")
        pe_xsT, act_xsT = sem("pe_xsT"), sem("act_xsT")
        dve_wc, pe_hA, pe_hB, act_hA, dve_hB = sem("dve_wc"), sem("pe_hA"), sem("pe_hB"), sem("act_hA"), sem("dve_hB")
        pe_y, dve_y = sem("pe_y"), sem("dve_y")
        dve_out = sem("dve_out")
        passed, passed_pool = sem("passed"), sem("passed_pool")
        dve_varc, act_lnc, act_rsc = sem("dve_varc"), sem("act_lnc"), sem("act_rsc")

        def wait(eng, s, v):
            if isinstance(v, int) and v <= 0:
                return
            eng.wait_ge(s, v)

        block = ctx.enter_context(nc.Block())

        N_SMALL = 11
        N_DCONST = 9
        LINKS_BATCH = 99
        LINKS_COMBINE = 29
        N_CONST = 8
        ZEROINGS = NG * SLOTS // (zero.shape[1] // H * P)

        @block.sync
        def _(sp):
            sp.dma_start(xhat2[:, 0:T, :], x_v[:, 0:T, :]).then_inc(x0_in, 16)

            def adj_load(b, h):
                wait(sp, dve_mask, (b - 1) * T + (h + 1) * (T // 2))
                src = adj_v[bass.ds(b, 1), :, :, h * HALF:(h + 1) * HALF]
                sp.dma_start(adj_st[:, h, :, :], src.rearrange("o p i j -> (o p) i j")).then_inc(adj_in[h], 16)

            for h in range(2):
                adj_load(0, h)
            sp.dma_start(xhat2[:, T:NT, :], x_v[:, T:NT, :]).then_inc(xr_in, 16)
            rows = zero.shape[1] // H * P
            for g in range(NG):
                zs_v = xs_d[g].rearrange("(z p r) d -> z p (r d)", p=P, r=rows // P)
                per = SLOTS // rows // 2
                with sp.Fori(1 + 2 * g, 3 + 2 * g) as b:
                    if g == 0:
                        sp.wait_ge(pool_const, N_CONST)
                    for z in range(per):
                        dst = zs_v[bass.ds((b - (1 + 2 * g)) * per + z, 1)]
                        sp.dma_start(dst.rearrange("o p c -> (o p) c"), zero[:]).then_inc(xs_zeroed, 16)
                    for h in range(2):
                        adj_load(b, h)
            with sp.Fori(1 + 2 * NG, NB) as b:
                for h in range(2):
                    adj_load(b, h)

            def xs_load(g, q, u):
                wait(sp, pe_xsT, g * (2 * NO) + q - 1)
                src = xs_d[g].rearrange("(q t p) d -> q p t d", t=QT, p=P)[bass.ds(q, 1)]
                sp.dma_start(xs[:, u, :, :], src.rearrange("o p t d -> (o p) t d")).then_inc(xs_in[u], 16)

            def y_store(g, q, u):
                sp.wait_ge(dve_y, (g * 2 * NO + q + 1) * QT)
                dst = y_d[g].rearrange("(q t p) d -> q p t d", t=QT, p=P)[bass.ds(q, 1)]
                sp.dma_start(dst.rearrange("o p t d -> (o p) t d"), ysb[:, u, :, :]).then_inc(y_out[u], 16)

            def out_store(c, u):
                sp.wait_ge(dve_out, c + 1)
                dst = out_v[:, bass.ds(c * QT, QT), :]
                sp.dma_start(dst, oc[:, u, :, :]).then_inc(o_out[u], 16)

            def oct_io(g, o):
                for u in range(2):
                    xs_load(g, 2 * o + u + 2, u)
                    y_store(g, 2 * o + u, u)

            lead = NO - CQ
            sp.wait_ge(dve_mask, NB * T)
            for g in range(NG):
                sp.wait_ge(scattered[g], 16 * KSEL * GT)
                xs_load(g, 0, 0)
                xs_load(g, 1, 1)
                if g == 0:
                    with sp.Fori(0, NO - 1) as o:
                        oct_io(g, o)
                else:
                    with sp.Fori(0, lead) as o:
                        oct_io(g, o)
                    with sp.Fori(0, CQ // 2 - 1) as c2:
                        for u in range(2):
                            oct_io(g, c2 * 2 + (lead + u))
                            out_store(c2 * 2 + u, u)
                    oct_io(g, NO - 2)
                    out_store(CQ - 2, 0)
                for u in range(2):
                    y_store(g, 2 * (NO - 1) + u, u)
            out_store(CQ - 1, 1)
            with sp.Fori(CQ // 2, CQ) as c2:
                for u in range(2):
                    out_store(c2 * 2 + u, u)
            for u in range(2):
                sp.wait_ge(o_out[u], 16 * NG * CQ // 2)
                sp.wait_ge(y_out[u], 16 * NG * NO)

        @block.gpsimd
        def _(pool):
            nc.gpsimd.memset(ident[:], 0.0).then_inc(pool_const, 1)
            nc.gpsimd.memset(tri[:], 1.0).then_inc(pool_const, 1)
            nc.gpsimd.memset(onesb[:], 1.0).then_inc(pool_const, 1)
            nc.gpsimd.memset(zero[:], 0.0).then_inc(pool_const, 1)
            nc.gpsimd.iota(iota_e[:], [[1, E]], base=0, channel_multiplier=0,
                           allow_small_or_imprecise_dtypes=True).then_inc(pool_const, 1)
            nc.gpsimd.iota(iota_s[:], [[1, S_T]], base=0, channel_multiplier=0,
                           allow_small_or_imprecise_dtypes=True).then_inc(pool_const, 1)
            pool.wait_ge(pool_const, 6)
            nc.gpsimd.affine_select(out=ident[:], in_=ident[:], compare_op=ALU.not_equal, fill=1.0,
                                    base=0, pattern=[[-1, P]], channel_multiplier=1).then_inc(pool_const, 1)
            nc.gpsimd.affine_select(out=tri[:], in_=tri[:], compare_op=ALU.is_gt, fill=0.0,
                                    base=0, pattern=[[1, P]], channel_multiplier=-1).then_inc(pool_const, 1)
            for g in range(NG):
                pool.wait_ge(dve_pos, g + 1)
                pool.wait_ge(act_xh2, (g + 1) * GB)
                if g == 0:
                    pool.wait_ge(xs_zeroed, 16 * ZEROINGS)
                for b in range(g * GB, (g + 1) * GB):
                    for t in range(T):
                        for k in range(KSEL):
                            pool.indirect_dma_start(
                                xs_d[g][:, :], bass.IndirectOffsetOnAxis(ap=pos[:, b, k, t:t + 1], axis=0),
                                xhat2[:, b * T + t, :], None).then_inc(scattered[g], 16)
            for g in range(NG):
                for u in range(2):
                    pool.wait_ge(y_out[u], 16 * NO * (g + 1))
                def gather_batch(n):
                    first = isinstance(n, int) and n == 0
                    for u in range(2):
                        if not first:
                            pool.wait_ge(gathered[u], n * (16 * QT * KSEL))
                            pool.wait_ge(dve_out, n * 2 - 1 + u)
                        nc.gpsimd.tensor_copy(
                            idxg[:, u, :, :],
                            pos[:, bass.ds(n, 1), :, u * QT:(u + 1) * QT]
                            .rearrange("p o k t -> p (o k) t")).then_inc(pool_idx, 1)
                        pool.wait_ge(pool_idx, n * 2 + u + 1)
                        pool.sem_inc(passed_pool, 1)
                        for t in range(QT):
                            for k in range(KSEL):
                                pool.indirect_dma_start(
                                    gath[:, u, t * KSEL + k, :], None, y_d[g][:, :],
                                    bass.IndirectOffsetOnAxis(ap=idxg[:, u, k, t:t + 1], axis=0)
                                ).then_inc(gathered[u], 16)

                if g == 0:
                    gather_batch(0)
                with pool.Fori(max(1, g * GB), (g + 1) * GB) as n:
                    gather_batch(n)

        @block.tensor
        def _(pe):
            pe.wait_ge(w_in, 16 * N_SMALL)
            pe.wait_ge(pool_const, N_CONST)
            for c in range(2):
                nc.tensor.matmul(GP[:, c * H:(c + 1) * H], zero[:, 0:P], wrel[c][:, 0, :],
                                 start=True, stop=True)
            nc.tensor.transpose(GP[:, 2 * H:2 * H + E * FH], b1rows[:], ident[0:E * FH, 0:E * FH]).then_inc(pe_b1, 1)

            def transposes(src, ready, per_tile, start, free, done):
                for u in range(2):
                    free(u)
                    wait(pe, ready, start + (u + 1) * per_tile)
                    for t in range(QT):
                        m = nc.tensor.transpose(TR[:, u, t * P:(t + 1) * P], src[:, u * QT + t, :], ident[:])
                    m.then_inc(done, 1)

            def project(c, srcT, ready, r0, idx):
                for u in range(2):
                    wait(pe, ready, r0 + u + 1)
                    wait(pe, dve_zlo, idx + u)
                    for t in range(QT):
                        n = (u * QT + t) * P
                        m = nc.tensor.matmul(ZB[:, t * H:(t + 1) * H], srcT[:, n:n + P], wrel[c][:, 1, :],
                                             start=True, stop=True)
                    m.then_inc(pe_z, 1)

            def aggregate(c, b, srcT, zready):
                wait(pe, dve_zlo, zready)
                for p in range(PAIRS):
                    idx = b * (2 * PAIRS) + c * PAIRS + p
                    wait(pe, dve_v, idx - 1)
                    for j in (2 * p, 2 * p + 1):
                        o = AG[:, 2 * (p % 2) + j % 2, :]
                        if c == 0:
                            pe.wait_ge(dve_mask, b * T + j + 1)
                        for i in range(T):
                            nc.tensor.matmul(o[:, 0:AGW], mask[:, j, i, :], zp[c][:, i, :],
                                             start=(i == 0), stop=(i == T - 1))
                        nc.tensor.matmul(o[:, 260:260 + H], srcT[:, j * P:(j + 1) * P], wroot[c][:],
                                         start=True, stop=False)
                        m = nc.tensor.matmul(o[:, 260:260 + H], ones2[:], bhl[:, c, :],
                                             start=False, stop=True)
                    m.then_inc(pe_ag, 1)

            def gate(b, free):
                transposes(x1b, dve_xh2, QT, b * T, free, pe_yT)
                pe.wait_ge(act_yT, 2 * b + 2)
                wait(pe, dve_rank, b)
                for t in range(T):
                    m = nc.tensor.matmul(GP[:, t * E:(t + 1) * E], yT[:, t * P:(t + 1) * P], gate_w[:],
                                         start=True, stop=True)
                m.then_inc(pe_gate, 1)

            def ranks(b, g):
                pe.wait_ge(dve_m1, b + 1)
                wait(pe, dve_carry, b)
                wait(pe, dve_pos, g)
                o = GP[:, T * E:2 * T * E].rearrange("p (t e) -> p t e", e=E)
                nc.tensor.matmul(o, tri[:], m1[:, :, :], start=True, stop=False)
                for t in range(T - 1):
                    nc.tensor.matmul(o[:, t + 1:T, :], onesb[:],
                                     m1[:, t:t + 1, :].broadcast_to([P, T - 1 - t, E]), start=False, stop=False)
                nc.tensor.matmul(o, onesb[:], carry[:].unsqueeze(1).broadcast_to([P, T, E]),
                                 start=False, stop=True).then_inc(pe_rank, 1)

            def counts(g):
                pe.wait_ge(dve_carry, (g + 1) * GB)
                pe.wait_ge(dve_rank, (g + 1) * GB)
                nc.tensor.matmul(GP[:, 2 * T * E:2 * T * E + E], onesb[:], carry[:],
                                 start=True, stop=True).then_inc(pe_cnt, 1)

            def batch(b, g, first=False, last=False):
                if first:
                    pe.wait_ge(dve_const, N_DCONST)
                aggregate(0, b, xT, 2 if first else b * 4)
                if not last:
                    transposes(xh1, dve_xh1, QT, (b + 1) * T, lambda u: wait(pe, act_hT, (b - 1) * 2 + u + 1), pe_xT)
                    project(0, xT, act_xT, (b + 1) * 2, b * 4 + 2)
                if not first:
                    gate(b - 1, lambda u: wait(pe, act_hT, (b - 1) * 2 + u + 1) if last
                         else wait(pe, act_xT, (b + 1) * 2 + u + 1))
                transposes(h1, dve_h, 2, b * 8,
                           lambda u: wait(pe, act_xT, (b + 1) * 2 + u + 1) if first
                           else wait(pe, act_yT, (b - 1) * 2 + u + 1), pe_hT)
                z = b * 4 + (2 if last else 4)
                project(1, hT, act_hT, b * 2, z)
                aggregate(1, b, hT, z + 2)
                if not first:
                    ranks(b - 1, g)

            transposes(xh1, dve_xh1, QT, 0, lambda u: None, pe_xT)
            project(0, xT, act_xT, 0, 0)
            batch(0, 0, first=True)
            with pe.Fori(1, GB + 1) as b:
                batch(b, 0)
            counts(0)
            with pe.Fori(GB + 1, NB - 1) as b:
                batch(b, 1)
            batch(NB - 1, 1, last=True)
            gate(NB - 1, lambda u: wait(pe, act_hT, (NB - 1) * 2 + u + 1))
            ranks(NB - 1, 1)
            counts(1)

            def slot_transposes(q, u):
                wait(pe, act_xsT, q - 1)
                pe.wait_ge(xs_in[u], (q - u) * 8 + 16)
                for t in range(QT):
                    m = nc.tensor.transpose(TR[:, u, t * P:(t + 1) * P], xs[:, u, t, :], ident[:])
                m.then_inc(pe_xsT, 1)

            def down(s, r):
                pe.wait_ge(act_hA, s + 1)
                pe.wait_ge(dve_hB, s + 1)
                wait(pe, dve_y, s - 1)
                for half, hh in enumerate((hA, hB)):
                    m = nc.tensor.matmul(YB[r % 2][:, 0:H], hh[:, r % 2, :],
                                         wc[:, r % 4, W2C + half * H:W2C + (half + 1) * H],
                                         start=(half == 0), stop=(half == 1))
                m.then_inc(pe_y, 1)

            def oct(o, first=False, last=False):
                for r in range(OCT):
                    u, t = r // QT, r % QT
                    if t == 0:
                        pe.wait_ge(act_xsT, o * 2 + u + 1)
                    s = o * OCT + r
                    pe.wait_ge(dve_wc, s + 1)
                    for half, (done, read) in enumerate(((pe_hA, act_hA), (pe_hB, dve_hB))):
                        wait(pe, read, s - 1)
                        nc.tensor.matmul(AG[:, 2 * half + r % 2, 0:P],
                                         wc[:, r % 4, half * P:(half + 1) * P],
                                         xsT[:, u, t * P:(t + 1) * P], start=True, stop=True).then_inc(done, 1)
                    if not (first and r == 0):
                        down(s - 1, (r - 1) % OCT)
                    if r == 2:
                        slot_transposes(o * 2 + 1, 1)
                    if r == 6 and not last:
                        slot_transposes(o * 2 + 2, 0)

            pe.wait_ge(dve_v, NB * 8)
            pe.wait_ge(act_yT, NB * 2)
            pe.wait_ge(dve_zlo, NB * 4)
            pe.wait_ge(dve_cnt, NG)
            for g in range(NG):
                slot_transposes(g * NO * 2, 0)
                oct(g * NO, first=True)
                with pe.Fori(g * NO + 1, (g + 1) * NO - 1) as o:
                    oct(o)
                oct((g + 1) * NO - 1, last=True)
                down((g + 1) * S_T - 1, OCT - 1)

        @block.scalar
        def _(act):
            small = [(wroot[0][:], w_root1_d), (wroot[1][:], w_root2_d),
                     (wrel[0][:], w_rel1_d.rearrange("r d e -> d r e")),
                     (wrel[1][:], w_rel2_d.rearrange("r d e -> d r e")),
                     (brow[0][:], b1g_d.partition_broadcast(P)), (brow[1][:], b2g_d.partition_broadcast(P)),
                     (gate_w[:], gate_w_d), (gate_b[:], gate_b_d.partition_broadcast(P)),
                     (gamma[:], gamma_d.partition_broadcast(P)), (beta[:], beta_d.partition_broadcast(P)),
                     (b1rows[:], b1_d.rearrange("e (c p) -> (e c) p", p=P))]
            assert len(small) == N_SMALL
            for dst, src in small:
                act.dma_start(dst, src).then_inc(w_in, 16)
            act.preload_act_table_set("natural_log_exp_and_others")
            act.wait_ge(pe_b1, 1)
            nc.scalar.activation(pack[:, :, B1C:B1C + FH],
                                 GP[:, 2 * H:2 * H + E * FH].rearrange("p (e c) -> p e c", c=FH),
                                 ACT.Copy).then_inc(act_b1, 1)
            act.wait_ge(adj_in[1], 16)
            act.dma_start(pack[:, :, 0:F], w1_d.rearrange("e h f -> h e f")).then_inc(pack_in, 16)
            w2_v = w2_d.rearrange("e (c p) h -> c p e h", p=P)
            for c in range(FH):
                act.dma_start(pack[:, :, W2C + c * H:W2C + (c + 1) * H], w2_v[c]).then_inc(pack_in, 16)
            act.dma_start(pack[:, :, B2C:B2C + H], b2_d.partition_broadcast(P)).then_inc(pack_in, 16)

            def rsqrt(var, ready, n, ln_out, out, s_ln, s_out):
                act.wait_ge(ready, n)
                nc.scalar.activation(ln_out, var, ACT.Ln, bias=epsb[:, 0:1]).then_inc(s_ln, 1)
                act.wait_ge(s_ln, n)
                nc.scalar.activation(out, ln_out, ACT.Exp, scale=-0.5).then_inc(s_out, 1)

            def rstd(n):
                rsqrt(mv[:, :, 1], dve_var, n, lnv[:], rs0[:], act_ln, act_rs)

            def evac(dst, ready, r0, done, base=None):
                for u in range(2):
                    act.wait_ge(ready, r0 + u + 1)
                    nc.scalar.activation(dst[:, u * 512:(u + 1) * 512], TR[:, u, :], ACT.Copy).then_inc(done, 1)

            def high(c, idx):
                for u in range(2):
                    act.wait_ge(pe_z, idx + u + 1)
                    nc.scalar.activation(zp[c][:, u * QT:(u + 1) * QT, 0:H],
                                         ZB[:].rearrange("p (t d) -> p t d", t=QT), ACT.Copy).then_inc(act_zhi, 1)

            def high_sum(idx, r):
                act.wait_ge(pe_ag, idx + 1)
                wait(act, dve_v, idx - 1)
                nc.scalar.activation(hs[:, r, :, :], AG[:, 2 * r:2 * r + 2, 0:H], ACT.Copy).then_inc(act_aghi, 1)

            def exps(idx, r):
                act.wait_ge(dve_v, idx + 1)
                wait(act, dve_h, idx - 1)
                nc.scalar.activation(ee[:, r, :, :], vv[:, r, :, :], ACT.Exp).then_inc(act_e, 1)

            def batch(b, first=False, last=False):
                high_sum(b * 8, 0)
                high_sum(b * 8 + 1, 1)
                exps(b * 8, 0)
                if not last:
                    rstd(b * 2 + 2)
                high_sum(b * 8 + 2, 0)
                exps(b * 8 + 1, 1)
                high_sum(b * 8 + 3, 1)
                exps(b * 8 + 2, 0)
                exps(b * 8 + 3, 1)
                if not last:
                    evac(xT, pe_xT, (b + 1) * 2, act_xT)
                    high(0, b * 4 + 2)
                if not first:
                    keep(b - 1)
                    evac(yT, pe_yT, (b - 1) * 2, act_yT)
                evac(hT, pe_hT, b * 2, act_hT)
                high(1, b * 4 + (2 if last else 4))
                high_sum(b * 8 + 4, 0)
                high_sum(b * 8 + 5, 1)
                exps(b * 8 + 4, 0)
                high_sum(b * 8 + 6, 0)
                exps(b * 8 + 5, 1)
                high_sum(b * 8 + 7, 1)
                exps(b * 8 + 6, 0)
                exps(b * 8 + 7, 1)
                rstd(b * 2 + (2 if last else 3))

            def keep(b):
                act.wait_ge(dve_xh2, (b + 1) * T)
                nc.scalar.activation(xhat2[:, bass.ds(b * T, T), :], x1b[:], ACT.Copy).then_inc(act_xh2, 1)

            def gate_exp(g):
                act.wait_ge(dve_gd, g + 1)
                nc.scalar.activation(gp[:], gq[:], ACT.Exp).then_inc(act_gp, 1)

            act.wait_ge(dve_const, 3)
            rstd(1)
            evac(xT, pe_xT, 0, act_xT)
            high(0, 0)
            batch(0, first=True)
            with act.Fori(1, GB + 1) as b:
                batch(b)
            gate_exp(0)
            with act.Fori(GB + 1, NB - 1) as b:
                batch(b)
            batch(NB - 1, last=True)
            keep(NB - 1)
            evac(yT, pe_yT, (NB - 1) * 2, act_yT)
            gate_exp(1)

            def slot_evac(q, u):
                act.wait_ge(pe_xsT, q + 1)
                wait(act, pe_hB, (q - 1) * QT)
                nc.scalar.activation(xsT[:, u, :], TR[:, u, :], ACT.Copy).then_inc(act_xsT, 1)

            def combine_rstd(c):
                rsqrt(mvc[:, :, 1], dve_varc, c + 1, lnc[:], rc0[:], act_lnc, act_rsc)

            def oct(o, last=False, combine=None):
                for r in range(OCT):
                    s = o * OCT + r
                    act.wait_ge(pe_hA, s + 1)
                    wait(act, pe_y, s - 1)
                    nc.scalar.activation(hA[:, r % 2, :], AG[:, r % 2, 0:P], ACT.Relu,
                                         bias=wc[:, r % 4, B1C:B1C + 1]).then_inc(act_hA, 1)
                    if r == 2:
                        slot_evac(o * 2 + 1, 1)
                    if r == 6 and not last:
                        slot_evac(o * 2 + 2, 0)
                    if r == 5 and combine is not None:
                        combine_rstd(combine)

            for g in range(NG):
                lead = NO - CQ if g else 0
                slot_evac(g * NO * 2, 0)
                if g == 0:
                    oct(0)
                    with act.Fori(1, NO - 1) as o:
                        oct(o)
                else:
                    with act.Fori(NO, NO + lead) as o:
                        oct(o)
                    with act.Fori(NO + lead, 2 * NO - 1) as o:
                        oct(o, combine=o - (NO + lead))
                oct((g + 1) * NO - 1, last=True, combine=CQ - 1 if g else None)
            with act.Fori(CQ, 2 * CQ) as c:
                combine_rstd(c)

        @block.vector
        def _(dve):
            class Self:
                base, n = 0, 0

                def link(self, ins):
                    ins.then_inc(dve_self, 1)
                    self.n += 1

                def wait(self):
                    dve.wait_ge(dve_self, self.base + self.n)

                def enter(self, i, start, per):
                    self.base0, self.n0 = self.base + self.n, per
                    self.base, self.n = (i - start) * per + self.base0, 0

                def leave(self, times):
                    assert self.n == self.n0, (self.n, self.n0)
                    self.base, self.n = self.base0 + times * self.n0, 0

            me = Self()

            def settled():
                me.wait()
                dve.sem_inc(passed, 1)

            link = me.link
            V = nc.vector

            V.memset(onez[:, 0:1], 1.0).then_inc(dve_const, 1)
            V.memset(onez[:, 1:2], 0.0).then_inc(dve_const, 1)
            V.memset(epsb[:], EPS).then_inc(dve_const, 1)
            link(V.memset(ones1[:], 1.0))
            link(V.memset(zer16[:], 0.0))
            link(V.memset(carryf[:], 0.0))
            V.memset(carry[:], 0.0).then_inc(dve_const, 1)
            V.memset(emap[0:1, NG * S_T:], 0).then_inc(dve_const, 1)
            dve.wait_ge(dve_const, 5)
            me.wait()
            for c in range(2):
                V.tensor_copy(zp[c][:, :, 2 * H:AGW], onez[:].unsqueeze(1).broadcast_to([P, T, 2]))\
                    .then_inc(dve_const, 1)
            V.tensor_copy(ones2[:], ones1[:]).then_inc(dve_const, 1)

            def ln_stats(src, halves=None):
                for t in range(T):
                    link(V.bn_stats(st[:, t, :], src(t)))

            def ln_var():
                settled()
                for t in range(T):
                    m = V.bn_aggr(mv[:, t, :], st[:, t, :])
                    if t < T - 1:
                        link(m)
                m.then_inc(dve_var, 1)

            def newton(r, s, var, ready, n):
                dve.wait_ge(ready, n)
                link(V.tensor_tensor(s, r, r, ALU.mult))
                me.wait()
                link(V.scalar_tensor_tensor(s, var, EPS, s, ALU.add, ALU.mult))
                me.wait()
                link(V.tensor_scalar(s, s, -0.5, 1.5, ALU.mult, ALU.add))
                me.wait()
                link(V.tensor_tensor(r, r, s, ALU.mult))
                me.wait()

            def ln_rstd(n):
                dve.wait_ge(dve_var, n)
                newton(rs0[:], rs1[:], mv[:, :, 1], act_rs, n)

            def ln_norm(dst, src, done):
                for t in range(T):
                    V.tensor_scalar(dst(t), src(t), mv[:, t, 0:1], rs0[:, t:t + 1],
                                    ALU.subtract, ALU.mult).then_inc(done, 1)

            def x_tile(b):
                return lambda t: xhat2[:, bass.ds(b * T + t, 1), :].rearrange("p o d -> p (o d)")

            def low(c, idx):
                for u in range(2):
                    dve.wait_ge(act_zhi, idx + u + 1)
                    q = slice(u * QT, (u + 1) * QT)
                    V.tensor_tensor(zp[c][:, q, H:2 * H], ZB[:].rearrange("p (t d) -> p t d", t=QT),
                                    zp[c][:, q, 0:H].bitcast(f32), ALU.subtract).then_inc(dve_zlo, 1)

            def convolved(idx, r):
                dve.wait_ge(act_aghi, idx + 1)
                ag = AG[:, 2 * r:2 * r + 2, :]
                link(V.tensor_scalar_max(dd[:, r], ag[:, :, 2 * H:2 * H + 1], 1.0))
                link(V.tensor_tensor(sm[:, r], ag[:, :, H:2 * H], hs[:, r, :, :], ALU.add))
                me.wait()
                link(V.reciprocal(rd[:, r], dd[:, r]))
                me.wait()
                wait(dve, act_e, idx - 1)
                for j in range(2):
                    m = V.scalar_tensor_tensor(vv[:, r, j, :], sm[:, r, j, :], rd[:, r, j, :],
                                               ag[:, j, 260:260 + H], ALU.mult, ALU.add)
                m.then_inc(dve_v, 1)

            def elu(idx, r):
                dve.wait_ge(act_e, idx + 1)
                link(V.tensor_scalar(mm_[:, r], ee[:, r, :, :], 1.0, -1.0, ALU.min, ALU.add))
                me.wait()

            def elu1(b, p):
                idx, r = b * 8 + p, p % 2
                elu(idx, r)
                V.scalar_tensor_tensor(h1[:, 2 * p:2 * p + 2, :], vv[:, r, :, :], 0.0, mm_[:, r],
                                       ALU.max, ALU.add).then_inc(dve_h, 1)

            def elu2(b, p, first):
                idx, r = b * 8 + 4 + p, p % 2
                elu(idx, r)
                q = slice(2 * p, 2 * p + 2)
                if not first and p == 0:
                    dve.wait_ge(pe_yT, b * 2)
                    dve.wait_ge(act_xh2, b)
                link(V.scalar_tensor_tensor(mm_[:, r], vv[:, r, :, :], 0.0, mm_[:, r], ALU.max, ALU.add))
                me.wait()
                V.tensor_tensor(x1b[:, q, :], mm_[:, r], xhat2[:, bass.ds(b * T + 2 * p, 2), :], ALU.add)\
                    .then_inc(dve_h, 1)

            def stats2(b, p):
                dve.wait_ge(dve_h, b * 8 + 5 + p)
                for t in (2 * p, 2 * p + 1):
                    link(V.bn_stats(st[:, t, :], x1b[:, t, :]))

            def make_mask(b, j):
                h = j // (T // 2)
                dve.wait_ge(adj_in[h], b * 16 + 16)
                n = j % (T // 2)
                V.tensor_scalar(mask[:, j, :, :], adj_st[:, h, :, n * P:(n + 1) * P], 1, None,
                                ALU.is_equal).then_inc(dve_mask, 1)

            def choose(b, g):
                dve.wait_ge(pe_gate, b + 1)
                link(V.tensor_tensor(logit[:], GP[:, 0:T * E].rearrange("p (t e) -> p t e", e=E),
                                     gate_b[:].unsqueeze(1).broadcast_to([P, T, E]), ALU.add))
                settled()
                for t in range(T):
                    link(V.max(top[:, t, :], logit[:, t, :]))
                settled()
                for t in range(T):
                    link(V.max_index(topi[:, t, :], top[:, t, :], logit[:, t, :]))
                link(V.tensor_copy(gates[:, bass.ds(b * T, T), :], top[:, :, 0:KSEL]))
                me.wait()
                link(V.tensor_copy(sel_e[:].rearrange("p k t -> p t k"), topi[:, :, 0:KSEL]))
                me.wait()
                oh = m12[:, bass.ds(b - g * GB, 1), :, :, :].rearrange("p o k t e -> p (o k t) e")
                link(V.tensor_tensor(
                    oh, iota_e[:].unsqueeze(1).broadcast_to([P, KSEL * T, E]),
                    sel_e[:].rearrange("p k t -> p (k t)").unsqueeze(2).broadcast_to([P, KSEL * T, E]),
                    ALU.is_equal))
                me.wait()
                oh4 = m12[:, bass.ds(b - g * GB, 1), :, :, :].rearrange("p o k t e -> p (o k) (t e)")
                V.tensor_tensor(m1[:].rearrange("p t e -> p (t e)"), oh4[:, 0, :], oh4[:, 1, :],
                                ALU.add).then_inc(dve_m1, 1)

            def take_ranks(b, g):
                dve.wait_ge(pe_rank, b + 1)
                oh = m12[:, bass.ds(b - g * GB, 1), :, :, :].rearrange("p o k t e -> p (o k) (t e)")
                V.tensor_tensor(rsel[:].rearrange("p k t e -> p k (t e)"), oh,
                                GP[:, T * E:2 * T * E].unsqueeze(1).broadcast_to([P, KSEL, T * E]),
                                ALU.mult).then_inc(dve_rank, 1)
                dve.wait_ge(dve_m1, b + 1)
                link(V.tensor_reduce(msum[:], m1[:].rearrange("p t e -> p e t"), AX.X, ALU.add))
                dve.wait_ge(dve_rank, b + 1)
                link(V.tensor_reduce(rank[:, bass.ds(b - g * GB, 1), :, :].rearrange("p o k t -> p (o k t)"),
                                     rsel[:].rearrange("p k t e -> p (k t) e"), AX.X, ALU.add))
                me.wait()
                link(V.tensor_tensor(carryf[:], carryf[:], msum[:], ALU.add))
                me.wait()
                V.tensor_copy(carry[:], carryf[:]).then_inc(dve_carry, 1)

            def place(g):
                dve.wait_ge(pe_cnt, g + 1)
                V.tensor_scalar(cnti[:], GP[:, 2 * T * E:2 * T * E + E], float(P - 1), None, ALU.add)\
                    .then_inc(dve_cnt, 1)
                dve.wait_ge(dve_cnt, g + 1)
                link(V.tensor_single_scalar(cntt[:], cnti[:], 7, ALU.logical_shift_right))
                me.wait()
                link(V.tensor_copy(ntl[:], cntt[:]))
                me.wait()
                link(V.tensor_tensor_scan(incl[:], ntl[:], zer16[:], 0.0, ALU.add, ALU.add))
                me.wait()
                link(V.tensor_tensor(base[:], incl[:], ntl[:], ALU.subtract))
                me.wait()
                link(V.tensor_scalar(base[:], base[:], float(P), None, ALU.mult))
                link(V.tensor_tensor(past[:], iota_s[:].unsqueeze(2).broadcast_to([1, S_T, E]),
                                     incl[0:1, :].unsqueeze(1).broadcast_to([1, S_T, E]), ALU.is_ge))
                me.wait()
                link(V.tensor_reduce(emf[:], past[:], AX.X, ALU.add))
                for n in range(GB):
                    link(V.tensor_tensor(rsel[:].rearrange("p k t e -> p (k t) e"),
                                         m12[:, n, :, :, :].rearrange("p k t e -> p (k t) e"),
                                         base[:].unsqueeze(1).broadcast_to([P, KSEL * T, E]), ALU.mult))
                    me.wait()
                    if n == 0:
                        link(V.tensor_scalar(emap[0:1, g * S_T:(g + 1) * S_T], emf[:], float(E - 1), None,
                                             ALU.min))
                    red = sel_e[:].rearrange("p k t -> p (k t)")
                    link(V.tensor_reduce(red, rsel[:].rearrange("p k t e -> p (k t) e"), AX.X, ALU.add))
                    me.wait()
                    m = V.tensor_tensor(pos[:, g * GB + n, :, :].rearrange("p k t -> p (k t)"), red,
                                        rank[:, n, :, :].rearrange("p k t -> p (k t)"), ALU.add)
                    if n < GB - 1:
                        link(m)
                        me.wait()
                gs = gates[:, g * GT:(g + 1) * GT, :]
                link(m)
                V.tensor_tensor(gq[:], gs[:, :, 1], gs[:, :, 0], ALU.subtract).then_inc(dve_gd, 1)
                dve.wait_ge(act_gp, g + 1)
                link(V.tensor_scalar(gq[:], gp[:], 1.0, None, ALU.add))
                me.wait()
                link(V.reciprocal(gs[:, :, 0], gq[:]))
                me.wait()
                link(V.tensor_tensor(gs[:, :, 1], gs[:, :, 0], gp[:], ALU.mult))
                link(V.memset(carryf[:], 0.0))
                me.wait()
                V.memset(carry[:], 0.0).then_inc(dve_pos, 1)

            def batch(b, g, first=False, last=False):
                convolved(b * 8, 0)
                if not last:
                    if first:
                        dve.wait_ge(xr_in, 16)
                    ln_stats(x_tile(b + 1))
                    ln_var()
                convolved(b * 8 + 1, 1)
                elu1(b, 0)
                if not last:
                    ln_rstd(b * 2 + 2)
                    if not first:
                        dve.wait_ge(pe_ag, b * 8)
                    ln_norm(lambda t: xh1[:, t, :], x_tile(b + 1), dve_xh1)
                convolved(b * 8 + 2, 0)
                elu1(b, 1)
                convolved(b * 8 + 3, 1)
                elu1(b, 2)
                elu1(b, 3)
                if not last:
                    low(0, b * 4 + 2)
                low(1, b * 4 + (2 if last else 4))
                for p in range(PAIRS):
                    convolved(b * 8 + 4 + p, p % 2)
                    if p == 0 and not first:
                        choose(b - 1, g)
                    if p:
                        elu2(b, p - 1, first)
                    if not last:
                        make_mask_pair(b, p)
                    if p:
                        stats2(b, p - 1)
                elu2(b, 3, first)
                stats2(b, 3)
                ln_var()
                n = b * 2 + (2 if last else 3)
                ln_rstd(n)
                link(V.scalar_tensor_tensor(std2[:, bass.ds(b * T, T)], mv[:, :, 1], EPS, rs0[:], ALU.add, ALU.mult))
                link(V.tensor_copy(mean2[:, bass.ds(b * T, T)], mv[:, :, 0]))
                ln_norm(lambda t: x1b[:, t, :], lambda t: x1b[:, t, :], dve_xh2)
                if not first:
                    take_ranks(b - 1, g)

            def make_mask_pair(b, p):
                for j in (2 * p, 2 * p + 1):
                    make_mask(b + 1, j)

            dve.wait_ge(x0_in, 16)
            ln_stats(lambda t: xhat2[:, t, :])
            ln_var()
            for j in range(T):
                make_mask(0, j)
            ln_rstd(1)
            ln_norm(lambda t: xh1[:, t, :], lambda t: xhat2[:, t, :], dve_xh1)
            dve.wait_ge(w_in, 16 * N_SMALL)
            dve.wait_ge(act_b1, 1)
            for c in range(2):
                link(V.tensor_tensor(biasf[:, c, :], GP[:, c * H:(c + 1) * H], brow[c][:], ALU.add))
            me.wait()
            link(V.tensor_copy(bhi[:], biasf[0:2, :, :]))
            me.wait()
            link(V.tensor_tensor(blo[:], biasf[0:2, :, :], bhi[:].bitcast(f32), ALU.subtract))
            dve.wait_ge(pool_const, N_CONST)
            me.wait()
            link(V.tensor_scalar(blo[:], blo[:], ident[0:2, 1:2], None, ALU.mult))
            me.wait()
            V.scalar_tensor_tensor(bhl[:], bhi[:].bitcast(f32), ident[0:2, 0:1], blo[:], ALU.mult, ALU.add)\
                .then_inc(dve_const, 1)
            low(0, 0)
            batch(0, 0, first=True)
            with dve.Fori(1, GB + 1) as b:
                me.enter(b, 1, LINKS_BATCH)
                batch(b, 0)
            me.leave(GB)
            place(0)
            with dve.Fori(GB + 1, NB - 1) as b:
                me.enter(b, GB + 1, LINKS_BATCH)
                batch(b, 1)
            me.leave(NB - 2 - GB)
            batch(NB - 1, 1, last=True)
            choose(NB - 1, 1)
            take_ranks(NB - 1, 1)
            place(1)

            def copy_weights(s, r, e):
                wait(dve, pe_y, s - 3)
                wait(dve, dve_y, s - 3)
                V.tensor_copy(wc[:, r % 4, :], pack[:, bass.ds(e, 1), :].rearrange("p o c -> p (o c)"))\
                    .then_inc(dve_wc, 1)

            def relu_high(s, r):
                dve.wait_ge(pe_hB, s + 1)
                wait(dve, pe_y, s - 1)
                V.tensor_scalar(hB[:, r % 2, :], AG[:, 2 + r % 2, 0:P], wc[:, r % 4, B1C + 1:B1C + 2], 0.0,
                                ALU.add, ALU.max).then_inc(dve_hB, 1)

            def result(s, r):
                u = r // QT
                dve.wait_ge(pe_y, s + 1)
                V.tensor_tensor(ysb[:, u, r % QT, :], YB[r % 2][:, 0:H], wc[:, r % 4, B2C:B2C + H],
                                ALU.add).then_inc(dve_y, 1)

            def experts_of(s):
                return nc.values_load_multi_w_load_instructions(
                    emap[0:1, bass.ds(s, OCT)], engines=(mybir.EngineType.DVE,), min_val=0, max_val=E - 1,
                    skip_runtime_bounds_check_because="place() clamps them to 0..E-1")[1]

            def combine1(c, u):
                dve.wait_ge(gathered[u], (c - u) * (8 * QT * KSEL) + 16 * QT * KSEL)
                wait(dve, dve_out, c)
                gt = [gates[:, bass.ds(c * QT + t, 1), :].rearrange("p o k -> p (o k)") for t in range(QT)]
                for t in range(QT):
                    link(V.scalar_tensor_tensor(
                        yc[:, t, :], gath[:, u, 2 * t, :], gt[t][:, 0:1],
                        xhat2[:, bass.ds(c * QT + t, 1), :].rearrange("p o d -> p (o d)"), ALU.mult, ALU.add))
                me.wait()
                for t in range(QT):
                    link(V.scalar_tensor_tensor(yc[:, t, :], gath[:, u, 2 * t + 1, :], gt[t][:, 1:2],
                                                yc[:, t, :], ALU.mult, ALU.add))
                me.wait()
                for t in range(QT):
                    link(V.bn_stats(stc[:, t, :], yc[:, t, :]))
                settled()
                for t in range(QT):
                    m = V.bn_aggr(mvc[:, t, :], stc[:, t, :])
                    if t < QT - 1:
                        link(m)
                m.then_inc(dve_varc, 1)
                for t in range(QT):
                    link(V.tensor_scalar(uc[:, t, :],
                                         xhat2[:, bass.ds(c * QT + t, 1), :].rearrange("p o d -> p (o d)"),
                                         std2[:, bass.ds(c * QT + t, 1)], mean2[:, bass.ds(c * QT + t, 1)],
                                         ALU.mult, ALU.add))
                me.wait()
                link(V.tensor_tensor(uc, uc, beta[:].unsqueeze(1).broadcast_to([P, QT, H]), ALU.add))

            def combine2(c, u, first=False):
                dve.wait_ge(dve_varc, c + 1)
                newton(rc0[:], rc1[:], mvc[:, :, 1], act_rsc, c + 1)
                for t in range(QT):
                    link(V.tensor_scalar(yc[:, t, :], yc[:, t, :], mvc[:, t, 0:1], rc0[:, t:t + 1],
                                         ALU.subtract, ALU.mult))
                me.wait()
                link(V.tensor_tensor(yc, yc, gamma[:].unsqueeze(1).broadcast_to([P, QT, H]), ALU.mult))
                me.wait()
                if not first:
                    dve.wait_ge(o_out[u], (c - u) * 8)
                V.tensor_tensor(oc[:, u, :, :], yc, uc, ALU.add).then_inc(dve_out, 1)

            def oct(o, first=False, combine=None):
                ex = experts_of(o * OCT + 2)
                for r in range(OCT):
                    s = o * OCT + r
                    copy_weights(s + 2, r + 2, ex[r])
                    relu_high(s, r)
                    if not (first and r == 0):
                        if r % QT == 1:
                            wait(dve, y_out[r // QT], o * 16)
                        result(s - 1, (r - 1) % OCT)
                    if combine is not None and r == 3:
                        combine1(*combine)
                    if combine is not None and r == 6:
                        combine2(*combine)

            ex = experts_of(0)
            dve.wait_ge(pack_in, 16 * (2 + FH))
            for r in range(2):
                copy_weights(r, r, ex[r])
            oct(0, first=True)
            with dve.Fori(1, NO) as o:
                oct(o)
            result(S_T - 1, OCT - 1)
            lead = NO - CQ
            oct(NO, first=True)
            with dve.Fori(NO + 1, NO + lead) as o:
                oct(o)
            for u in range(2):
                oct(NO + lead + u, combine=(u, u))
            with dve.Fori(1, CQ // 2) as c2:
                me.enter(c2, 1, 2 * LINKS_COMBINE)
                for u in range(2):
                    oct(c2 * 2 + (NO + lead + u), combine=(c2 * 2 + u, u))
            me.leave(CQ // 2 - 1)
            result(2 * S_T - 1, OCT - 1)
            with dve.Fori(CQ // 2, CQ) as c2:
                me.enter(c2, CQ // 2, 2 * LINKS_COMBINE)
                for u in range(2):
                    combine1(c2 * 2 + u, u)
                    combine2(c2 * 2 + u, u)
            me.leave(CQ // 2)


_INS = ["x", "adj", "L0_gnn_w_rel1", "L0_gnn_w_root1", "L0_gnn_b1", "L0_gnn_w_rel2", "L0_gnn_w_root2",
        "L0_gnn_b2", "L0_ffn_gate_w", "L0_ffn_gate_b", "L0_ffn_w1", "L0_ffn_b1", "L0_ffn_w2", "L0_ffn_b2",
        "L0_ffn_gamma", "L0_ffn_beta"]
_OUTS = [((8, 1024, 128), "float32")]


def kernel(**inputs):
    import numpy as _np
    import concourse.bacc as _bacc
    from concourse import mybir as _mybir
    from concourse.bass_utils import run_bass_kernel_spmd as _run

    nc = _bacc.Bacc("TRN2", target_bir_lowering=False, num_devices=1)
    arrays, args = {}, []
    for name in _INS:
        a = _np.ascontiguousarray(inputs[name])
        arrays[f"in_{name}"] = a
        args.append(nc.dram_tensor(f"in_{name}", a.shape, _mybir.dt.from_np(a.dtype), kind="ExternalInput").ap())
    for i, (shape, dtype) in enumerate(_OUTS):
        dt = _mybir.dt.from_np(_np.dtype(dtype))
        args.append(nc.dram_tensor(f"out_{i}", shape, dt, kind="ExternalOutput").ap())
    gnn_moe_kernel(nc, *args)
    r = _run(nc, [arrays], core_ids=[0])
    return r.results[0]["out_0"]
```

```python
import concourse.bass as bass
from concourse import mybir
from contextlib import ExitStack


def gnn_moe_kernel(nc, x_d, adj_d, w_rel1_d, w_root1_d, b1g_d, w_rel2_d, w_root2_d, b2g_d,
                   gate_w_d, gate_b_d, w1_d, b1_d, w2_d, b2_d, gamma_d, beta_d, out_d):
    f32, f32r = mybir.dt.float32, mybir.dt.float32r
    bf16, i32, u32 = mybir.dt.bfloat16, mybir.dt.int32, mybir.dt.uint32
    ALU = mybir.AluOpType
    ACT = mybir.ActivationFunctionType
    AX = mybir.AxisListType

    NB, N, H = x_d.shape
    E, _, F = w1_d.shape
    P = 128
    T = N // P
    NT = NB * T
    KSEL = 2
    FH = F // P
    EPS = 1e-5
    NG = 2
    GB = NB // NG
    GT = GB * T
    OCT = 8
    S_T = -(-(GT * KSEL + E - 1) // OCT) * OCT
    NO = S_T // OCT
    SLOTS = S_T * P
    QT = 4
    PAIRS = T // 2
    CQ = GT // QT
    W2C, B1C, B2C = F, F + FH * H, F + FH * H + FH
    PACK = F + FH * H + FH + H
    PW = N // PAIRS
    AGW = 2 * H + 2

    x_v = x_d.rearrange("b (t p) d -> p (b t) d", p=P)
    out_v = out_d.rearrange("b (t p) d -> p (b t) d", p=P)
    adj_v = adj_d.rearrange("b (i p) j -> b p i j", p=P)
    xs_d = [nc.dram_tensor(f"expert_inputs_{g}", (SLOTS, H), f32).ap() for g in range(NG)]
    y_d = [nc.dram_tensor(f"expert_outputs_{g}", (SLOTS, H), f32).ap() for g in range(NG)]

    ctx = ExitStack()
    with ctx:
        def sb(name, shape, dt=f32):
            return ctx.enter_context(nc.sbuf_tensor(name, shape, dt))

        def pb(name, shape, dt=f32):
            return ctx.enter_context(nc.psum_tensor(name, shape, dt))

        def sem(name):
            return ctx.enter_context(nc.semaphore(name))

        xhat2 = sb("xhat2", [P, NT, H])
        mean2 = sb("mean2", [P, NT])
        std2 = sb("std2", [P, NT])
        gates = sb("gates", [P, NT, KSEL])
        pos = sb("pos", [P, NB, KSEL, T], i32)
        emap = sb("emap", [1, NG * S_T + OCT], i32)
        ident = sb("ident", [P, P])
        gamma = sb("gamma", [P, H])
        beta = sb("beta", [P, H])
        b1c = sb("b1c", [P, E, FH])
        xh1 = sb("xh1", [P, T, H])
        xT = sb("xT", [P, N])
        h1 = sb("h1", [P, T, H])
        hT = sb("hT", [P, N])
        x1b = sb("x1b", [P, T, H])
        xn2 = sb("xn2", [P, T, H])
        yT = sb("yT", [P, N])
        zp = [sb(f"zp{c}", [P, T, AGW], f32r) for c in (1, 2)]
        hs = sb("hs", [P, 2, 2, H])
        sm = sb("sm", [P, 2, 2, H])
        vv = sb("vv", [P, 2, 2, H])
        ee = sb("ee", [P, 2, 2, H])
        mm_ = sb("mm_", [P, 2, 2, H])
        deg = sb("deg", [P, T, 1])
        rdeg = [sb(f"rdeg{k}", [P, T, 1]) for k in range(2)]
        wroot = [sb(f"wroot{c}", [P, H]) for c in (1, 2)]
        wrel = [sb(f"wrel{c}", [P, 2, H]) for c in (1, 2)]
        brow = [sb(f"brow{c}", [P, H]) for c in (1, 2)]
        biasf = sb("biasf", [P, 2, H])
        bhl = sb("bhl", [2, 2, H], f32r)
        ones2 = sb("ones2", [2, P], f32r)
        onez = sb("onez", [P, 2])
        b1rows = sb("b1rows", [E * FH, P])
        bhi = sb("bhi", [2, 2, H], f32r)
        blo = sb("blo", [2, 2, H])
        ones1 = sb("ones1", [2, P])
        zero = sb("zero", [P, 4 * P])
        epsb = sb("epsb", [P, 1])
        neg1 = sb("neg1", [P, 1])
        st = [sb(f"st{k}", [P, T, 6]) for k in (1, 2)]
        mv = [sb(f"mv{k}", [P, T, 2]) for k in (1, 2)]
        lnv = [sb(f"lnv{k}", [P, T]) for k in (1, 2)]
        rstd = [sb(f"rstd{k}", [P, T]) for k in (1, 2)]
        nwt = [sb(f"nwt{k}", [P, T]) for k in (1, 2)]
        nmr = [sb(f"nmr{k}", [P, T]) for k in (1, 2)]
        gate_w = sb("gate_w", [P, E])
        gate_b = sb("gate_b", [P, E])
        logit = sb("logit", [P, T, E])
        top = sb("top", [P, T, 8])
        topi = sb("topi", [P, T, 8], u32)
        sel_e = sb("sel_e", [P, KSEL, T])
        iota_e = sb("iota_e", [P, E])
        iota_s = sb("iota_s", [1, S_T])
        m12 = sb("m12", [P, GB, KSEL, T, E], bf16)
        m1 = sb("m1", [P, T, E], bf16)
        carry = sb("carry", [P, E], bf16)
        carryf = sb("carryf", [P, E])
        msum = sb("msum", [P, E])
        tri = sb("tri", [P, P], bf16)
        onesb = sb("onesb", [P, P], bf16)
        rsel = sb("rsel", [P, KSEL, T, E])
        rank = sb("rank", [P, GB, KSEL, T])
        cnti = sb("cnti", [P, E], i32)
        cntt = sb("cntt", [P, E], i32)
        ntl = sb("ntl", [P, E])
        incl = sb("incl", [P, E])
        base = sb("base", [P, E])
        zer16 = sb("zer16", [P, E])
        past = sb("past", [1, S_T, E], bf16)
        emf = sb("emf", [1, S_T])
        gq = sb("gq", [P, GT])
        gp = sb("gp", [P, GT])
        with ExitStack() as graph_phase:
            mask = [graph_phase.enter_context(nc.sbuf_tensor("mask_even", [P, T, T, P], f32r)), None]
            adj_st = graph_phase.enter_context(nc.sbuf_tensor("adj_st", [P, 2, T, PW], i32))
            mask[1] = graph_phase.enter_context(nc.sbuf_tensor("mask_odd", [P, T, T, P], f32r))
        pack = sb("pack", [P, E, PACK])
        xs = sb("xs", [P, 2, QT, H])
        xsT = sb("xsT", [P, 2, QT * P])
        wc = sb("wc", [P, 4, PACK])
        ysb = sb("ysb", [P, 2, QT, H])
        gath = sb("gath", [P, 2, QT * KSEL, H])
        hA, hB = hs[:, 0, :, :], hs[:, 1, :, :]
        idxg = sb("idxg", [P, 2, KSEL, QT], i32)
        stc = sb("stc", [P, QT, 6])
        mvc = sb("mvc", [P, QT, 2])
        lnc = sb("lnc", [P, QT])
        rc0 = sb("rc0", [P, QT])
        rc1 = sb("rc1", [P, QT])
        nmc = sb("nmc", [P, QT])
        yc = xh1[:, 0:QT, :]
        uc = xh1[:, QT:2 * QT, :]
        oc = h1[:, :, :].rearrange("p (u t) d -> p u t d", u=2)

        AG = pb("AG", [P, 4, 512])
        TR = pb("TR", [P, 3, 512])
        GP = pb("GP", [P, 512])
        YB = [TR[:, 2, :], GP[:, :]]

        w_in = sem("w_in")
        pack_in = sem("pack_in")
        x0_in, xr_in = sem("x0_in"), sem("xr_in")
        adj_in = [sem(f"adj_in{u}") for u in range(2)]
        xs_zeroed = sem("xs_zeroed")
        scattered = [sem(f"scattered{g}") for g in range(NG)]
        xs_in = [sem(f"xs_in{u}") for u in range(2)]
        y_out = [sem(f"y_out{u}") for u in range(2)]
        gathered = [sem(f"gathered{u}") for u in range(2)]
        o_out = [sem(f"o_out{u}") for u in range(2)]
        pool_const = sem("pool_const")
        pool_idx = sem("pool_idx")
        dve_const = sem("dve_const")
        dve_self = sem("dve_self")
        pe_bias, pe_b1 = sem("pe_bias"), sem("pe_b1")
        act_b1, act_pack = sem("act_b1"), sem("act_pack")
        pe_xT, pe_hT, pe_yT = sem("pe_xT"), sem("pe_hT"), sem("pe_yT")
        act_xT, act_hT, act_yT = sem("act_xT"), sem("act_hT"), sem("act_yT")
        pe_z, act_zhi, dve_zlo = sem("pe_z"), sem("act_zhi"), sem("dve_zlo")
        pe_ag, act_aghi, dve_v = sem("pe_ag"), sem("act_aghi"), sem("dve_v")
        act_e, dve_h = sem("act_e"), sem("dve_h")
        dve_mask, pool_mask = sem("dve_mask"), sem("pool_mask")
        dve_var = [sem(f"dve_var{k}") for k in (1, 2)]
        act_ln = [sem(f"act_ln{k}") for k in (1, 2)]
        act_rs = [sem(f"act_rs{k}") for k in (1, 2)]
        dve_rstd = [sem(f"dve_rstd{k}") for k in (1, 2)]
        act_xh1, act_xh2 = sem("act_xh1"), sem("act_xh2")
        xh2_kept = sem("xh2_kept")
        pe_gate, dve_m1, pe_rank, dve_rank = sem("pe_gate"), sem("dve_m1"), sem("pe_rank"), sem("dve_rank")
        dve_carry = sem("dve_carry")
        pe_cnt, dve_cnt, dve_pos = sem("pe_cnt"), sem("dve_cnt"), sem("dve_pos")
        dve_gd, act_gp = sem("dve_gd"), sem("act_gp")
        pe_xsT, act_xsT = sem("pe_xsT"), sem("act_xsT")
        dve_wc, pe_up, act_h = sem("dve_wc"), sem("pe_up"), sem("act_h")
        pe_y, dve_y = sem("pe_y"), sem("dve_y")
        dve_out = sem("dve_out")
        passed, passed_pool = sem("passed"), sem("passed_pool")
        dve_varc, act_lnc, act_rsc = sem("dve_varc"), sem("act_lnc"), sem("act_rsc")
        dve_rstdc, act_x1c, act_nc = sem("dve_rstdc"), sem("act_x1c"), sem("act_nc")

        def wait(eng, s, v):
            if isinstance(v, int) and v <= 0:
                return
            eng.wait_ge(s, v)

        def pair_no(c, i, p):
            if isinstance(i, int) and i == 0:
                return p
            if isinstance(i, int) and i == NB:
                return 2 * PAIRS * NB - PAIRS + p
            return i * (2 * PAIRS) - PAIRS * (1 - c) + p

        def z_no(c, b, u):
            if c == 0:
                return u if isinstance(b, int) and b == 0 else b * 4 - 2 + u
            return NB * 4 - 2 + u if isinstance(b, int) and b == NB - 1 else b * 4 + 4 + u

        block = ctx.enter_context(nc.Block())

        N_SMALL = 11
        N_DCONST = 10
        LINKS_STEPS = 166
        LINKS_COMBINE = 21
        N_CONST = 8
        ZEROINGS = NG * SLOTS // (zero.shape[1] // H * P)

        @block.sync
        def _(sp):
            sp.dma_start(xhat2[:, 0:T, :], x_v[:, 0:T, :]).then_inc(x0_in, 16)

            def adj_load(b, p):
                wait(sp, dve_mask, b * PAIRS + p - 1)
                wait(sp, pool_mask, b * PAIRS + p - 1)
                src = adj_v[bass.ds(b, 1), :, :, p * PW:(p + 1) * PW]
                sp.dma_start(adj_st[:, p % 2, :, :], src.rearrange("o p i j -> (o p) i j"))\
                    .then_inc(adj_in[p % 2], 16)

            def keep(b):
                sp.wait_ge(act_xh2, (b + 1) * T)
                sp.dma_start(xhat2[:, bass.ds(b * T, T), :].rearrange("p t d -> p (t d)"),
                             xn2[:].rearrange("p t d -> p (t d)")).then_inc(xh2_kept, 16)

            def clear(g, n):
                rows = zero.shape[1] // H * P
                zs_v = xs_d[g].rearrange("(z p r) d -> z p (r d)", p=P, r=rows // P)
                for z in range(SLOTS // rows // GB):
                    dst = zs_v[bass.ds(n * (SLOTS // rows // GB) + z, 1)]
                    sp.dma_start(dst.rearrange("o p c -> (o p) c"), zero[:]).then_inc(xs_zeroed, 16)

            def step_loads(b, cleared, kept=True):
                for p in range(2):
                    adj_load(b, p)
                clear(*cleared)
                if kept:
                    keep(b - 3)
                for p in range(2, PAIRS):
                    adj_load(b, p)

            for p in range(PAIRS):
                adj_load(0, p)
            sp.dma_start(xhat2[:, T:NT, :], x_v[:, T:NT, :]).then_inc(xr_in, 16)
            sp.wait_ge(pool_const, N_CONST)
            for b in (1, 2):
                step_loads(b, (0, b - 1), kept=False)
            with sp.Fori(3, GB + 1) as b:
                step_loads(b, (0, b - 1))
            with sp.Fori(GB + 1, NB) as b:
                step_loads(b, (1, b - (GB + 1)))
            clear(1, GB - 1)
            keep(NB - 3)
            sp.wait_ge(pe_ag, pair_no(1, NB - 1, PAIRS))
            sp.wait_ge(dve_mask, NB * PAIRS)
            sp.wait_ge(pool_mask, NB * PAIRS)
            sp.dma_start(pack[:, :, 0:F], w1_d.rearrange("e h f -> h e f")).then_inc(pack_in, 16)
            w2_v = w2_d.rearrange("e (c p) h -> c p e h", p=P)
            for c in range(FH):
                sp.dma_start(pack[:, :, W2C + c * H:W2C + (c + 1) * H], w2_v[c]).then_inc(pack_in, 16)
            sp.dma_start(pack[:, :, B2C:B2C + H], b2_d.partition_broadcast(P)).then_inc(pack_in, 16)
            keep(NB - 2)
            keep(NB - 1)

            def xs_load(g, q, u):
                wait(sp, pe_xsT, g * (2 * NO) + q - 1)
                src = xs_d[g].rearrange("(q t p) d -> q p t d", t=QT, p=P)[bass.ds(q, 1)]
                sp.dma_start(xs[:, u, :, :], src.rearrange("o p t d -> (o p) t d")).then_inc(xs_in[u], 16)

            def y_store(g, q, u):
                sp.wait_ge(dve_y, (g * 2 * NO + q + 1) * QT)
                dst = y_d[g].rearrange("(q t p) d -> q p t d", t=QT, p=P)[bass.ds(q, 1)]
                sp.dma_start(dst.rearrange("o p t d -> (o p) t d"), ysb[:, u, :, :]).then_inc(y_out[u], 16)

            def out_store(c, u):
                sp.wait_ge(dve_out, c + 1)
                dst = out_v[:, bass.ds(c * QT, QT), :]
                sp.dma_start(dst, oc[:, u, :, :]).then_inc(o_out[u], 16)

            def oct_io(g, o):
                for u in range(2):
                    xs_load(g, 2 * o + u + 2, u)
                    y_store(g, 2 * o + u, u)

            lead = NO - CQ
            sp.wait_ge(pe_ag, 2 * NB * PAIRS)
            for g in range(NG):
                sp.wait_ge(scattered[g], 16 * KSEL * GT)
                xs_load(g, 0, 0)
                xs_load(g, 1, 1)
                if g == 0:
                    with sp.Fori(0, NO - 1) as o:
                        oct_io(g, o)
                else:
                    with sp.Fori(0, lead) as o:
                        oct_io(g, o)
                    with sp.Fori(0, CQ // 2 - 1) as c2:
                        for u in range(2):
                            oct_io(g, c2 * 2 + (lead + u))
                            out_store(c2 * 2 + u, u)
                    oct_io(g, NO - 2)
                    out_store(CQ - 2, 0)
                for u in range(2):
                    y_store(g, 2 * (NO - 1) + u, u)
            out_store(CQ - 1, 1)
            with sp.Fori(CQ // 2, CQ) as c2:
                for u in range(2):
                    out_store(c2 * 2 + u, u)
            for u in range(2):
                sp.wait_ge(o_out[u], 16 * NG * CQ // 2)
                sp.wait_ge(y_out[u], 16 * NG * NO)

        @block.gpsimd
        def _(pool):
            nc.gpsimd.memset(ident[:], 0.0).then_inc(pool_const, 1)
            nc.gpsimd.memset(tri[:], 1.0).then_inc(pool_const, 1)
            nc.gpsimd.memset(onesb[:], 1.0).then_inc(pool_const, 1)
            nc.gpsimd.memset(zero[:], 0.0).then_inc(pool_const, 1)
            nc.gpsimd.iota(iota_e[:], [[1, E]], base=0, channel_multiplier=0,
                           allow_small_or_imprecise_dtypes=True).then_inc(pool_const, 1)
            nc.gpsimd.iota(iota_s[:], [[1, S_T]], base=0, channel_multiplier=0,
                           allow_small_or_imprecise_dtypes=True).then_inc(pool_const, 1)
            pool.wait_ge(pool_const, 6)
            nc.gpsimd.affine_select(out=ident[:], in_=ident[:], compare_op=ALU.not_equal, fill=1.0,
                                    base=0, pattern=[[-1, P]], channel_multiplier=1).then_inc(pool_const, 1)
            nc.gpsimd.affine_select(out=tri[:], in_=tri[:], compare_op=ALU.is_gt, fill=0.0,
                                    base=0, pattern=[[1, P]], channel_multiplier=-1).then_inc(pool_const, 1)

            def masks(b, parity):
                for p in range(PAIRS):
                    pool.wait_ge(adj_in[p % 2], b * 32 + (p // 2 + 1) * 16)
                    if not isinstance(b, int):
                        pool.wait_ge(pe_ag, pair_no(1, b - 1, p) + 1)
                        pool.sem_inc(passed_pool, 1)
                    nc.gpsimd.tensor_scalar(mask[parity][:, 2 * p + 1, :, :], adj_st[:, p % 2, :, P:2 * P],
                                            1, None, ALU.is_equal).then_inc(pool_mask, 1)

            for b in range(2):
                masks(b, b)
            with pool.Fori(1, NB // 2) as k:
                for parity in range(2):
                    masks(k * 2 + parity, parity)

            for g in range(NG):
                pool.wait_ge(dve_pos, g + 1)
                pool.wait_ge(xh2_kept, 16 * (g + 1) * GB)
                if g == 0:
                    pool.wait_ge(xs_zeroed, 16 * ZEROINGS)
                for b in range(g * GB, (g + 1) * GB):
                    for t in range(T):
                        for k in range(KSEL):
                            pool.indirect_dma_start(
                                xs_d[g][:, :], bass.IndirectOffsetOnAxis(ap=pos[:, b, k, t:t + 1], axis=0),
                                xhat2[:, b * T + t, :], None).then_inc(scattered[g], 16)
            for g in range(NG):
                for u in range(2):
                    pool.wait_ge(y_out[u], 16 * NO * (g + 1))
                def gather_batch(n):
                    first = isinstance(n, int) and n == 0
                    for u in range(2):
                        if not first:
                            pool.wait_ge(gathered[u], n * (16 * QT * KSEL))
                            pool.wait_ge(dve_out, n * 2 - 1 + u)
                        nc.gpsimd.tensor_copy(
                            idxg[:, u, :, :],
                            pos[:, bass.ds(n, 1), :, u * QT:(u + 1) * QT]
                            .rearrange("p o k t -> p (o k) t")).then_inc(pool_idx, 1)
                        pool.wait_ge(pool_idx, n * 2 + u + 1)
                        pool.sem_inc(passed_pool, 1)
                        for t in range(QT):
                            for k in range(KSEL):
                                pool.indirect_dma_start(
                                    gath[:, u, t * KSEL + k, :], None, y_d[g][:, :],
                                    bass.IndirectOffsetOnAxis(ap=idxg[:, u, k, t:t + 1], axis=0)
                                ).then_inc(gathered[u], 16)

                if g == 0:
                    gather_batch(0)
                with pool.Fori(max(1, g * GB), (g + 1) * GB) as n:
                    gather_batch(n)

        @block.tensor
        def _(pe):
            pe.wait_ge(w_in, 16 * N_SMALL)
            pe.wait_ge(pool_const, N_CONST)
            for c in range(2):
                nc.tensor.matmul(GP[:, c * H:(c + 1) * H], zero[:, 0:P], wrel[c][:, 0, :],
                                 start=True, stop=True)
            nc.tensor.transpose(GP[:, 2 * H:2 * H + E * FH], b1rows[:], ident[0:E * FH, 0:E * FH]).then_inc(pe_b1, 1)

            def transposes(src, u, bank, done):
                for t in range(QT):
                    m = nc.tensor.transpose(TR[:, bank, t * P:(t + 1) * P], src[:, u * QT + t, :], ident[:])
                m.then_inc(done, 1)

            def project(c, u, srcT, bank):
                for t in range(QT):
                    n = (u * QT + t) * P
                    m = nc.tensor.matmul(TR[:, bank, t * H:(t + 1) * H], srcT[:, n:n + P],
                                         wrel[c][:, 1, :], start=True, stop=True)
                m.then_inc(pe_z, 1)

            def aggregate(c, i, p, srcT, parity):
                b = i - c
                if p == 0:
                    pe.wait_ge(dve_zlo, z_no(c, b, 1) + 1)
                if c == 0:
                    pe.wait_ge(dve_mask, b * PAIRS + p + 1)
                    pe.wait_ge(pool_mask, b * PAIRS + p + 1)
                wait(pe, dve_v, pair_no(c, i, p) - 1)
                width = AGW if c == 0 else 2 * H
                for j in (2 * p, 2 * p + 1):
                    o = AG[:, 2 * (p % 2) + j % 2, :]
                    for k in range(T):
                        nc.tensor.matmul(o[:, 0:width], mask[parity][:, j, k, :], zp[c][:, k, 0:width],
                                         start=(k == 0), stop=(k == T - 1))
                    nc.tensor.matmul(o[:, 260:260 + H], srcT[:, j * P:(j + 1) * P], wroot[c][:],
                                     start=True, stop=False)
                    m = nc.tensor.matmul(o[:, 260:260 + H], ones2[:], bhl[:, c, :],
                                         start=False, stop=True)
                m.then_inc(pe_ag, 1)

            def gate(b):
                pe.wait_ge(act_yT, b * 2 + 2)
                wait(pe, dve_rank, b)
                for t in range(T):
                    m = nc.tensor.matmul(GP[:, t * E:(t + 1) * E], yT[:, t * P:(t + 1) * P], gate_w[:],
                                         start=True, stop=True)
                m.then_inc(pe_gate, 1)

            def ranks(b, g):
                pe.wait_ge(dve_m1, b + 1)
                wait(pe, dve_carry, b)
                wait(pe, dve_pos, g)
                o = GP[:, T * E:2 * T * E].rearrange("p (t e) -> p t e", e=E)
                nc.tensor.matmul(o, tri[:], m1[:, :, :], start=True, stop=False)
                for t in range(T - 1):
                    nc.tensor.matmul(o[:, t + 1:T, :], onesb[:],
                                     m1[:, t:t + 1, :].broadcast_to([P, T - 1 - t, E]), start=False, stop=False)
                nc.tensor.matmul(o, onesb[:], carry[:].unsqueeze(1).broadcast_to([P, T, E]),
                                 start=False, stop=True).then_inc(pe_rank, 1)

            def counts(g):
                pe.wait_ge(dve_carry, (g + 1) * GB)
                pe.wait_ge(dve_rank, (g + 1) * GB)
                nc.tensor.matmul(GP[:, 2 * T * E:2 * T * E + E], onesb[:], carry[:],
                                 start=True, stop=True).then_inc(pe_cnt, 1)

            def transpose_y(b, u):
                pe.wait_ge(act_xh2, b * T + (u + 1) * QT)
                transposes(xn2, u, 1 + u, pe_yT)

            def step(i, parity):
                at = i if isinstance(i, int) else 3
                conv1, conv2 = at < NB, at > 0
                for p in range(PAIRS):
                    if conv1:
                        aggregate(0, i, p, xT, parity)
                    if conv2 and p < 2:
                        pe.wait_ge(act_hT, (i - 1) * 2 + p + 1)
                        if p == 0:
                            if at > 2:
                                pe.wait_ge(act_yT, (i - 3) * 2 + 2)
                            if at < NB:
                                pe.wait_ge(dve_zlo, z_no(0, i, 0) + 1)
                        project(1, p, hT, 2 if p == 0 else 0)
                for p in range(PAIRS):
                    if conv2:
                        aggregate(1, i, p, hT, 1 - parity)
                    if p == 0 and at < NB - 1:
                        if conv2:
                            pe.wait_ge(dve_zlo, z_no(1, i - 1, 1) + 1)
                        else:
                            pe.wait_ge(dve_zlo, z_no(0, 0, 1) + 1)
                        for u in range(2):
                            if u == 1 and conv2:
                                pe.wait_ge(act_hT, (i - 1) * 2 + 2)
                            pe.wait_ge(act_xh1, (i + 1) * T + (u + 1) * QT)
                            transposes(xh1, u, u, pe_xT)
                    if p == 0 and at > 2:
                        ranks(i - 3, 0 if at <= GB + 2 else 1)
                    if p in (1, 2) and at < NB - 1:
                        pe.wait_ge(act_xT, (i + 1) * 2 + p)
                        if p == 1 and conv2:
                            pe.wait_ge(dve_zlo, z_no(1, i - 1, 0) + 1)
                        project(0, p - 1, xT, 2 if p == 1 else 0)
                    if p == 2 and at > 1:
                        if at < NB - 1:
                            pe.wait_ge(act_xT, (i + 1) * 2 + 2)
                        else:
                            pe.wait_ge(act_hT, i * 2)
                        transpose_y(i - 2, 0)
                        pe.wait_ge(dve_zlo, (z_no(0, i + 1, 0) if at < NB - 1 else z_no(1, i - 1, 0)) + 1)
                        transpose_y(i - 2, 1)
                if at > 1:
                    gate(i - 2)
                if conv1:
                    for u in range(2):
                        pe.wait_ge(dve_h, pair_no(0, i, 2 * u + 1) + 1)
                        if u == 0:
                            pe.wait_ge(dve_zlo, (z_no(0, i + 1, 1) if at < NB - 1 else z_no(1, i - 1, 1)) + 1)
                        elif at > 1:
                            pe.wait_ge(act_yT, (i - 2) * 2 + 1)
                        elif at == 0 or at == 1:
                            pe.wait_ge(act_xT, (i + 1) * 2 + 2)
                        transposes(h1, u, u, pe_hT)

            pe.wait_ge(dve_const, N_DCONST)
            for u in range(2):
                pe.wait_ge(act_xh1, (u + 1) * QT)
                transposes(xh1, u, u, pe_xT)
            for u in range(2):
                pe.wait_ge(act_xT, u + 1)
                project(0, u, xT, 2 if u == 0 else 0)
            for i in range(3):
                step(i, i % 2)
            with pe.Fori(1, (NB - 2) // 2) as k:
                step(k * 2 + 1, 1)
                step(k * 2 + 2, 0)
            counts(0)
            for i in (NB - 1, NB):
                step(i, i % 2)
            ranks(NB - 2, 1)
            pe.wait_ge(dve_zlo, NB * 4)
            pe.wait_ge(act_yT, (NB - 1) * 2)
            for u in range(2):
                transpose_y(NB - 1, u)
            gate(NB - 1)
            ranks(NB - 1, 1)
            counts(1)

            def slot_transposes(q, u):
                wait(pe, act_xsT, q - 1)
                pe.wait_ge(xs_in[u], (q - u) * 8 + 16)
                for t in range(QT):
                    m = nc.tensor.transpose(TR[:, u, t * P:(t + 1) * P], xs[:, u, t, :], ident[:])
                m.then_inc(pe_xsT, 1)

            def down(s, r):
                pe.wait_ge(act_h, s + 1)
                wait(pe, dve_y, s - 1)
                for half, hh in enumerate((hA, hB)):
                    m = nc.tensor.matmul(YB[r % 2][:, 0:H], hh[:, r % 2, :],
                                         wc[:, r % 4, W2C + half * H:W2C + (half + 1) * H],
                                         start=(half == 0), stop=(half == 1))
                m.then_inc(pe_y, 1)

            def oct(o, first=False, last=False):
                for r in range(OCT):
                    u, t = r // QT, r % QT
                    if t == 0:
                        pe.wait_ge(act_xsT, o * 2 + u + 1)
                    s = o * OCT + r
                    pe.wait_ge(dve_wc, s + 1)
                    wait(pe, act_h, s - 3)
                    for half in range(FH):
                        m = nc.tensor.matmul(AG[:, r % 4, half * P:(half + 1) * P],
                                             wc[:, r % 4, half * P:(half + 1) * P],
                                             xsT[:, u, t * P:(t + 1) * P], start=True, stop=True)
                    m.then_inc(pe_up, 1)
                    if not (first and r == 0):
                        down(s - 1, (r - 1) % OCT)
                    if r == 2:
                        slot_transposes(o * 2 + 1, 1)
                    if r == 6 and not last:
                        slot_transposes(o * 2 + 2, 0)

            pe.wait_ge(dve_v, 2 * NB * PAIRS)
            pe.wait_ge(act_yT, NB * 2)
            pe.wait_ge(dve_cnt, NG)
            for g in range(NG):
                slot_transposes(g * NO * 2, 0)
                oct(g * NO, first=True)
                with pe.Fori(g * NO + 1, (g + 1) * NO - 1) as o:
                    oct(o)
                oct((g + 1) * NO - 1, last=True)
                down((g + 1) * S_T - 1, OCT - 1)

        @block.scalar
        def _(act):
            small = [(wroot[0][:], w_root1_d), (wroot[1][:], w_root2_d),
                     (wrel[0][:], w_rel1_d.rearrange("r d e -> d r e")),
                     (wrel[1][:], w_rel2_d.rearrange("r d e -> d r e")),
                     (brow[0][:], b1g_d.partition_broadcast(P)), (brow[1][:], b2g_d.partition_broadcast(P)),
                     (gate_w[:], gate_w_d), (gate_b[:], gate_b_d.partition_broadcast(P)),
                     (gamma[:], gamma_d.partition_broadcast(P)), (beta[:], beta_d.partition_broadcast(P)),
                     (b1rows[:], b1_d.rearrange("e (c p) -> (e c) p", p=P))]
            assert len(small) == N_SMALL
            for dst, src in small:
                act.dma_start(dst, src).then_inc(w_in, 16)
            act.preload_act_table_set("natural_log_exp_and_others")
            act.wait_ge(pe_b1, 1)
            nc.scalar.activation(b1c[:], GP[:, 2 * H:2 * H + E * FH].rearrange("p (e c) -> p e c", c=FH),
                                 ACT.Copy).then_inc(act_b1, 1)

            def rsqrt(var, ready, n, ln_out, out, s_ln, s_out):
                act.wait_ge(ready, n)
                nc.scalar.activation(ln_out, var, ACT.Ln, bias=epsb[:, 0:1]).then_inc(s_ln, 1)
                act.wait_ge(s_ln, n)
                nc.scalar.activation(out, ln_out, ACT.Exp, scale=-0.5).then_inc(s_out, 1)

            def ln_rsqrt(k, b):
                rsqrt(mv[k][:, :, 1], dve_var[k], b + 1, lnv[k][:], rstd[k][:], act_ln[k], act_rs[k])

            def norm(k, b, u, dst, done, src):
                act.wait_ge(dve_rstd[k], b + 1)
                for t in range(u * QT, (u + 1) * QT):
                    nc.scalar.activation(dst[:, t, :], src(t), ACT.Identity, scale=rstd[k][:, t:t + 1],
                                         bias=nmr[k][:, t:t + 1]).then_inc(done, 1)

            def x_tile(b):
                return lambda t: xhat2[:, bass.ds(b * T + t, 1), :].rearrange("p o d -> p (o d)")

            def layernorm1(b, u):
                wait(act, pe_xT, b * 2)
                norm(0, b, u, xh1, act_xh1, x_tile(b))

            def layernorm2(b, u):
                wait(act, pe_yT, b * 2)
                wait(act, xh2_kept, b * 16)
                norm(1, b, u, xn2, act_xh2, lambda t: x1b[:, t, :])

            def evac(dst, u, bank, ready, r, done, less_one=False):
                act.wait_ge(ready, r)
                o, i = dst[:, u * 512:(u + 1) * 512], TR[:, bank, :]
                if less_one:
                    m = nc.scalar.activation(o, i, ACT.Identity, bias=neg1[:, 0:1])
                else:
                    m = nc.scalar.activation(o, i, ACT.Copy)
                m.then_inc(done, 1)

            def high(c, b, u):
                act.wait_ge(pe_z, z_no(c, b, u) + 1)
                nc.scalar.activation(zp[c][:, u * QT:(u + 1) * QT, 0:H],
                                     TR[:, 2 if u == 0 else 0, :].rearrange("p (t d) -> p t d", t=QT), ACT.Copy)\
                    .then_inc(act_zhi, 1)

            def high_sum(n, r):
                act.wait_ge(pe_ag, n + 1)
                wait(act, dve_v, n - 1)
                nc.scalar.activation(hs[:, r, :, :], AG[:, 2 * r:2 * r + 2, 0:H], ACT.Copy).then_inc(act_aghi, 1)

            def exps(n, r):
                act.wait_ge(dve_v, n + 1)
                wait(act, dve_h, n - 1)
                nc.scalar.activation(ee[:, r, :, :], vv[:, r, :, :], ACT.Exp, bias=neg1[:, 0:1]).then_inc(act_e, 1)

            def y_evac(b, u):
                wait(act, pe_gate, b)
                evac(yT, u, 1 + u, pe_yT, b * 2 + u + 1, act_yT)

            def step(i):
                at = i if isinstance(i, int) else 3
                conv1, conv2, more = at < NB, at > 0, at < NB - 1
                for p in range(PAIRS):
                    if conv1:
                        high_sum(pair_no(0, i, p), p % 2)
                    if p == 0 and more:
                        ln_rsqrt(0, i + 1)
                    if p == 1 and at > 1:
                        ln_rsqrt(1, i - 2)
                    if p < 2 and conv2:
                        high(1, i - 1, p)
                    if conv1:
                        exps(pair_no(0, i, p), p % 2)
                    if p in (1, 2) and more:
                        layernorm1(i + 1, p - 1)
                    if p == 3 and at > 1:
                        layernorm2(i - 2, 0)
                for p in range(PAIRS):
                    if conv2:
                        high_sum(pair_no(1, i, p), p % 2)
                    if p == 0 and more:
                        for u in range(2):
                            evac(xT, u, u, pe_xT, (i + 1) * 2 + u + 1, act_xT)
                    if p in (1, 2) and more:
                        high(0, i + 1, p - 1)
                    if conv2:
                        exps(pair_no(1, i, p), p % 2)
                    if p == 0 and at > 1:
                        layernorm2(i - 2, 1)
                    if p == 2 and at > 1:
                        for u in range(2):
                            y_evac(i - 2, u)
                if conv1:
                    for u in range(2):
                        evac(hT, u, u, pe_hT, i * 2 + u + 1, act_hT, True)

            def gate_exp(g):
                act.wait_ge(dve_gd, g + 1)
                nc.scalar.activation(gp[:], gq[:], ACT.Exp).then_inc(act_gp, 1)

            act.wait_ge(dve_const, 4)
            ln_rsqrt(0, 0)
            for u in range(2):
                layernorm1(0, u)
            for u in range(2):
                evac(xT, u, u, pe_xT, u + 1, act_xT)
            for u in range(2):
                high(0, 0, u)
            for i in range(3):
                step(i)
            with act.Fori(1, (NB - 2) // 2) as k:
                step(k * 2 + 1)
                step(k * 2 + 2)
            gate_exp(0)
            for i in (NB - 1, NB):
                step(i)
            ln_rsqrt(1, NB - 1)
            for u in range(2):
                layernorm2(NB - 1, u)
            for u in range(2):
                y_evac(NB - 1, u)
            gate_exp(1)
            act.wait_ge(pack_in, 16 * (2 + FH))
            nc.scalar.activation(pack[:, :, B1C:B1C + FH], b1c[:], ACT.Copy).then_inc(act_pack, 1)

            def slot_evac(q, u):
                act.wait_ge(pe_xsT, q + 1)
                wait(act, pe_up, (q - 1) * QT)
                nc.scalar.activation(xsT[:, u, :], TR[:, u, :], ACT.Copy).then_inc(act_xsT, 1)

            def combine(c):
                wait(act, dve_out, c)
                for t in range(QT):
                    nc.scalar.activation(uc[:, t, :], xhat2[:, bass.ds(c * QT + t, 1), :].rearrange("p o d -> p (o d)"),
                                         ACT.Identity, scale=std2[:, bass.ds(c * QT + t, 1)],
                                         bias=mean2[:, bass.ds(c * QT + t, 1)]).then_inc(act_x1c, 1)
                rsqrt(mvc[:, :, 1], dve_varc, c + 1, lnc[:], rc0[:], act_lnc, act_rsc)

            def combine_norm(c):
                act.wait_ge(dve_rstdc, c + 1)
                for t in range(QT):
                    nc.scalar.activation(yc[:, t, :], yc[:, t, :], ACT.Identity, scale=rc0[:, t:t + 1],
                                         bias=nmc[:, t:t + 1]).then_inc(act_nc, 1)

            def oct(o, last=False, combined=None):
                for r in range(OCT):
                    s = o * OCT + r
                    act.wait_ge(pe_up, s + 1)
                    wait(act, pe_y, s - 1)
                    for half, hh in enumerate((hA, hB)):
                        m = nc.scalar.activation(hh[:, r % 2, :], AG[:, r % 4, half * P:(half + 1) * P],
                                                 ACT.Relu, bias=wc[:, r % 4, B1C + half:B1C + half + 1])
                    m.then_inc(act_h, 1)
                    if r == 2:
                        slot_evac(o * 2 + 1, 1)
                    if r == 6 and not last:
                        slot_evac(o * 2 + 2, 0)
                    if combined is not None and r == 4:
                        combine(combined)
                    if combined is not None and r == 6:
                        combine_norm(combined)

            for g in range(NG):
                lead = NO - CQ if g else 0
                slot_evac(g * NO * 2, 0)
                if g == 0:
                    oct(0)
                    with act.Fori(1, NO - 1) as o:
                        oct(o)
                else:
                    with act.Fori(NO, NO + lead) as o:
                        oct(o)
                    with act.Fori(NO + lead, 2 * NO - 1) as o:
                        oct(o, combined=o - (NO + lead))
                oct((g + 1) * NO - 1, last=True, combined=CQ - 1 if g else None)
            with act.Fori(CQ, 2 * CQ) as c:
                combine(c)
                combine_norm(c)

        @block.vector
        def _(dve):
            class Self:
                base, n = 0, 0

                def link(self, ins):
                    ins.then_inc(dve_self, 1)
                    self.n += 1
                    return self.n

                def wait(self, n=None):
                    dve.wait_ge(dve_self, self.base + (self.n if n is None else n))

                def enter(self, i, start, per):
                    self.base0, self.n0 = self.base + self.n, per
                    self.base, self.n = (i - start) * per + self.base0, 0

                def leave(self, times):
                    assert self.n == self.n0, (self.n, self.n0)
                    self.base, self.n = self.base0 + times * self.n0, 0

            me = Self()

            def settled():
                me.wait()
                dve.sem_inc(passed, 1)

            link = me.link
            V = nc.vector

            V.memset(onez[:, 0:1], 1.0).then_inc(dve_const, 1)
            V.memset(onez[:, 1:2], 0.0).then_inc(dve_const, 1)
            V.memset(epsb[:], EPS).then_inc(dve_const, 1)
            V.memset(neg1[:], -1.0).then_inc(dve_const, 1)
            link(V.memset(ones1[:], 1.0))
            link(V.memset(zer16[:], 0.0))
            link(V.memset(carryf[:], 0.0))
            V.memset(carry[:], 0.0).then_inc(dve_const, 1)
            V.memset(emap[0:1, NG * S_T:], 0).then_inc(dve_const, 1)
            dve.wait_ge(dve_const, 6)
            me.wait()
            for c in range(2):
                V.tensor_copy(zp[c][:, :, 2 * H:AGW], onez[:].unsqueeze(1).broadcast_to([P, T, 2]))\
                    .then_inc(dve_const, 1)
            V.tensor_copy(ones2[:], ones1[:]).then_inc(dve_const, 1)

            def ln_stats(k, src, tiles=range(T)):
                for t in tiles:
                    link(V.bn_stats(st[k][:, t, :], src(t)))

            def ln_var(k):
                settled()
                for t in range(T):
                    m = V.bn_aggr(mv[k][:, t, :], st[k][:, t, :])
                    if t < T - 1:
                        link(m)
                m.then_inc(dve_var[k], 1)

            def newton(r, s, var, ready, n):
                dve.wait_ge(ready, n)
                link(V.tensor_tensor(s, r, r, ALU.mult))
                me.wait()
                link(V.scalar_tensor_tensor(s, var, EPS, s, ALU.add, ALU.mult))
                me.wait()
                link(V.tensor_scalar(s, s, -0.5, 1.5, ALU.mult, ALU.add))
                me.wait()
                link(V.tensor_tensor(r, r, s, ALU.mult))
                me.wait()

            def ln_rstd(k, b):
                dve.wait_ge(dve_var[k], b + 1)
                newton(rstd[k][:], nwt[k][:], mv[k][:, :, 1], act_rs[k], b + 1)
                V.scalar_tensor_tensor(nmr[k][:], mv[k][:, :, 0], -1.0, rstd[k][:], ALU.mult, ALU.mult)\
                    .then_inc(dve_rstd[k], 1)

            def x_tile(b):
                return lambda t: xhat2[:, bass.ds(b * T + t, 1), :].rearrange("p o d -> p (o d)")

            def low(c, b, u):
                dve.wait_ge(act_zhi, z_no(c, b, u) + 1)
                q = slice(u * QT, (u + 1) * QT)
                V.tensor_tensor(zp[c][:, q, H:2 * H], TR[:, 2 if u == 0 else 0, :].rearrange("p (t d) -> p t d", t=QT),
                                zp[c][:, q, 0:H].bitcast(f32), ALU.subtract).then_inc(dve_zlo, 1)

            def convolved(c, i, p, parity, between=None):
                idx, r, q = pair_no(c, i, p), p % 2, slice(2 * p, 2 * p + 2)
                dve.wait_ge(act_aghi, idx + 1)
                ag = AG[:, 2 * r:2 * r + 2, :]
                if c == 0:
                    n = link(V.tensor_scalar_max(deg[:, q], ag[:, :, 2 * H:2 * H + 1], 1.0))
                m = link(V.tensor_tensor(sm[:, r], ag[:, :, H:2 * H], hs[:, r, :, :], ALU.add))
                if c == 0:
                    me.wait(n)
                    m = link(V.reciprocal(rdeg[parity][:, q], deg[:, q]))
                if between is not None:
                    between()
                wait(dve, act_e, idx - 1)
                me.wait(m)
                for j in range(2):
                    m = V.scalar_tensor_tensor(vv[:, r, j, :], sm[:, r, j, :], rdeg[parity][:, 2 * p + j, :],
                                               ag[:, j, 260:260 + H], ALU.mult, ALU.add)
                m.then_inc(dve_v, 1)

            def elu1(i, p):
                r = p % 2
                dve.wait_ge(act_e, pair_no(0, i, p) + 1)
                wait(dve, pe_hT, i * 2)
                V.scalar_tensor_tensor(h1[:, 2 * p:2 * p + 2, :], ee[:, r, :, :], 1.0, vv[:, r, :, :],
                                       ALU.min, ALU.max).then_inc(dve_h, 1)

            def elu2(i, p):
                r = p % 2
                dve.wait_ge(act_e, pair_no(1, i, p) + 1)
                n = link(V.scalar_tensor_tensor(mm_[:, r], ee[:, r, :, :], 1.0, vv[:, r, :, :], ALU.min, ALU.max))
                wait(dve, act_xh2, (i - 1) * T)
                me.wait(n)
                V.scalar_tensor_tensor(x1b[:, 2 * p:2 * p + 2, :], mm_[:, r], -1.0,
                                       xhat2[:, bass.ds((i - 1) * T + 2 * p, 2), :], ALU.add, ALU.add)\
                    .then_inc(dve_h, 1)

            def stats2(i, p):
                dve.wait_ge(dve_h, pair_no(1, i, p) + 1)
                ln_stats(1, lambda t: x1b[:, t, :], (2 * p, 2 * p + 1))

            def ln_rstd2(b):
                ln_rstd(1, b)
                link(V.scalar_tensor_tensor(std2[:, bass.ds(b * T, T)], mv[1][:, :, 1], EPS, rstd[1][:],
                                            ALU.add, ALU.mult))
                link(V.tensor_copy(mean2[:, bass.ds(b * T, T)], mv[1][:, :, 0]))

            def make_mask(b, p, parity):
                dve.wait_ge(adj_in[p % 2], b * 32 + (p // 2 + 1) * 16)
                if not (isinstance(b, int) and b < 2):
                    dve.wait_ge(pe_ag, pair_no(1, b - 1, p) + 1)
                V.tensor_scalar(mask[parity][:, 2 * p, :, :], adj_st[:, p % 2, :, 0:P], 1, None,
                                ALU.is_equal).then_inc(dve_mask, 1)

            def choose(b):
                dve.wait_ge(pe_gate, b + 1)
                link(V.tensor_tensor(logit[:], GP[:, 0:T * E].rearrange("p (t e) -> p t e", e=E),
                                     gate_b[:].unsqueeze(1).broadcast_to([P, T, E]), ALU.add))
                settled()
                for t in range(T):
                    link(V.max(top[:, t, :], logit[:, t, :]))
                settled()
                for t in range(T):
                    link(V.max_index(topi[:, t, :], top[:, t, :], logit[:, t, :]))
                link(V.tensor_copy(gates[:, bass.ds(b * T, T), :], top[:, :, 0:KSEL]))

            def choose_onehot(b, g):
                me.wait()
                link(V.tensor_copy(sel_e[:].rearrange("p k t -> p t k"), topi[:, :, 0:KSEL]))
                me.wait()
                oh = m12[:, bass.ds(b - g * GB, 1), :, :, :].rearrange("p o k t e -> p (o k t) e")
                link(V.tensor_tensor(
                    oh, iota_e[:].unsqueeze(1).broadcast_to([P, KSEL * T, E]),
                    sel_e[:].rearrange("p k t -> p (k t)").unsqueeze(2).broadcast_to([P, KSEL * T, E]),
                    ALU.is_equal))
                me.wait()
                oh4 = m12[:, bass.ds(b - g * GB, 1), :, :, :].rearrange("p o k t e -> p (o k) (t e)")
                V.tensor_tensor(m1[:].rearrange("p t e -> p (t e)"), oh4[:, 0, :], oh4[:, 1, :],
                                ALU.add).then_inc(dve_m1, 1)

            def take_ranks(b, g):
                dve.wait_ge(pe_rank, b + 1)
                oh = m12[:, bass.ds(b - g * GB, 1), :, :, :].rearrange("p o k t e -> p (o k) (t e)")
                V.tensor_tensor(rsel[:].rearrange("p k t e -> p k (t e)"), oh,
                                GP[:, T * E:2 * T * E].unsqueeze(1).broadcast_to([P, KSEL, T * E]),
                                ALU.mult).then_inc(dve_rank, 1)
                dve.wait_ge(dve_m1, b + 1)
                link(V.tensor_reduce(msum[:], m1[:].rearrange("p t e -> p e t"), AX.X, ALU.add))
                dve.wait_ge(dve_rank, b + 1)
                link(V.tensor_reduce(rank[:, bass.ds(b - g * GB, 1), :, :].rearrange("p o k t -> p (o k t)"),
                                     rsel[:].rearrange("p k t e -> p (k t) e"), AX.X, ALU.add))
                me.wait()
                link(V.tensor_tensor(carryf[:], carryf[:], msum[:], ALU.add))
                me.wait()
                V.tensor_copy(carry[:], carryf[:]).then_inc(dve_carry, 1)

            def place(g):
                dve.wait_ge(pe_cnt, g + 1)
                V.tensor_scalar(cnti[:], GP[:, 2 * T * E:2 * T * E + E], float(P - 1), None, ALU.add)\
                    .then_inc(dve_cnt, 1)
                dve.wait_ge(dve_cnt, g + 1)
                link(V.tensor_single_scalar(cntt[:], cnti[:], 7, ALU.logical_shift_right))
                me.wait()
                link(V.tensor_copy(ntl[:], cntt[:]))
                me.wait()
                link(V.tensor_tensor_scan(incl[:], ntl[:], zer16[:], 0.0, ALU.add, ALU.add))
                me.wait()
                link(V.tensor_tensor(base[:], incl[:], ntl[:], ALU.subtract))
                me.wait()
                link(V.tensor_scalar(base[:], base[:], float(P), None, ALU.mult))
                link(V.tensor_tensor(past[:], iota_s[:].unsqueeze(2).broadcast_to([1, S_T, E]),
                                     incl[0:1, :].unsqueeze(1).broadcast_to([1, S_T, E]), ALU.is_ge))
                me.wait()
                link(V.tensor_reduce(emf[:], past[:], AX.X, ALU.add))
                for n in range(GB):
                    link(V.tensor_tensor(rsel[:].rearrange("p k t e -> p (k t) e"),
                                         m12[:, n, :, :, :].rearrange("p k t e -> p (k t) e"),
                                         base[:].unsqueeze(1).broadcast_to([P, KSEL * T, E]), ALU.mult))
                    me.wait()
                    if n == 0:
                        link(V.tensor_scalar(emap[0:1, g * S_T:(g + 1) * S_T], emf[:], float(E - 1), None,
                                             ALU.min))
                    red = sel_e[:].rearrange("p k t -> p (k t)")
                    link(V.tensor_reduce(red, rsel[:].rearrange("p k t e -> p (k t) e"), AX.X, ALU.add))
                    me.wait()
                    m = V.tensor_tensor(pos[:, g * GB + n, :, :].rearrange("p k t -> p (k t)"), red,
                                        rank[:, n, :, :].rearrange("p k t -> p (k t)"), ALU.add)
                    if n < GB - 1:
                        link(m)
                        me.wait()
                gs = gates[:, g * GT:(g + 1) * GT, :]
                link(m)
                V.tensor_tensor(gq[:], gs[:, :, 1], gs[:, :, 0], ALU.subtract).then_inc(dve_gd, 1)
                dve.wait_ge(act_gp, g + 1)
                link(V.tensor_scalar(gq[:], gp[:], 1.0, None, ALU.add))
                me.wait()
                link(V.reciprocal(gs[:, :, 0], gq[:]))
                me.wait()
                link(V.tensor_tensor(gs[:, :, 1], gs[:, :, 0], gp[:], ALU.mult))
                link(V.memset(carryf[:], 0.0))
                me.wait()
                V.memset(carry[:], 0.0).then_inc(dve_pos, 1)

            def step(i, parity):
                at = i if isinstance(i, int) else 3
                conv1, conv2, more, g = at < NB, at > 0, at < NB - 1, 0 if at <= GB + 2 else 1
                if conv1 and conv2:
                    make_mask(i, PAIRS - 1, parity)
                if more:
                    if at == 0:
                        dve.wait_ge(xr_in, 16)
                    ln_stats(0, x_tile(i + 1))
                    ln_var(0)
                if conv1:
                    convolved(0, i, 0, parity)
                if at > 1:
                    ln_var(1)
                if more:
                    ln_rstd(0, i + 1)
                if conv2:
                    low(1, i - 1, 0)
                if conv1:
                    convolved(0, i, 1, parity, lambda: elu1(i, 0))
                if conv2:
                    low(1, i - 1, 1)
                if at > 1:
                    ln_rstd2(i - 2)
                if conv1:
                    convolved(0, i, 2, parity, lambda: elu1(i, 1))
                if at > 2:
                    choose(i - 3)
                if conv1:
                    convolved(0, i, 3, parity, lambda: elu1(i, 2))
                if at > 2:
                    choose_onehot(i - 3, g)
                last_elu1 = lambda: elu1(i, 3) if conv1 else None
                if not conv2:
                    last_elu1()
                for p in range(PAIRS):
                    if conv2:
                        convolved(1, i, p, 1 - parity, (lambda: elu2(i, p - 1)) if p else last_elu1)
                        if p:
                            stats2(i, p - 1)
                    if p in (1, 2) and more:
                        low(0, i + 1, p - 1)
                    if p < PAIRS - 1 and more:
                        make_mask(i + 1, p, 1 - parity)
                    if p == 2 and at > 2:
                        take_ranks(i - 3, g)
                if conv2:
                    elu2(i, PAIRS - 1)
                    stats2(i, PAIRS - 1)

            dve.wait_ge(x0_in, 16)
            ln_stats(0, lambda t: xhat2[:, t, :])
            ln_var(0)
            for p in range(PAIRS):
                make_mask(0, p, 0)
            ln_rstd(0, 0)
            dve.wait_ge(w_in, 16 * N_SMALL)
            dve.wait_ge(act_b1, 1)
            for c in range(2):
                link(V.tensor_tensor(biasf[:, c, :], GP[:, c * H:(c + 1) * H], brow[c][:], ALU.add))
            me.wait()
            link(V.tensor_scalar(biasf[:], biasf[:], 1.0, None, ALU.add))
            me.wait()
            link(V.tensor_copy(bhi[:], biasf[0:2, :, :]))
            me.wait()
            link(V.tensor_tensor(blo[:], biasf[0:2, :, :], bhi[:].bitcast(f32), ALU.subtract))
            dve.wait_ge(pool_const, N_CONST)
            me.wait()
            link(V.tensor_scalar(blo[:], blo[:], ident[0:2, 1:2], None, ALU.mult))
            me.wait()
            V.scalar_tensor_tensor(bhl[:], bhi[:].bitcast(f32), ident[0:2, 0:1], blo[:], ALU.mult, ALU.add)\
                .then_inc(dve_const, 1)
            for u in range(2):
                low(0, 0, u)
            for i in range(3):
                step(i, i % 2)
            with dve.Fori(1, (NB - 2) // 2) as k:
                me.enter(k, 1, LINKS_STEPS)
                step(k * 2 + 1, 1)
                step(k * 2 + 2, 0)
            me.leave((NB - 2) // 2 - 1)
            place(0)
            for i in (NB - 1, NB):
                step(i, i % 2)
            ln_var(1)
            ln_rstd2(NB - 1)
            for b in (NB - 2, NB - 1):
                choose(b)
                choose_onehot(b, 1)
                take_ranks(b, 1)
            place(1)

            def copy_weights(s, r, e):
                wait(dve, pe_y, s - 3)
                wait(dve, dve_y, s - 3)
                V.tensor_copy(wc[:, r % 4, :], pack[:, bass.ds(e, 1), :].rearrange("p o c -> p (o c)"))\
                    .then_inc(dve_wc, 1)

            def result(s, r):
                u = r // QT
                dve.wait_ge(pe_y, s + 1)
                V.tensor_tensor(ysb[:, u, r % QT, :], YB[r % 2][:, 0:H], wc[:, r % 4, B2C:B2C + H],
                                ALU.add).then_inc(dve_y, 1)

            def experts_of(s):
                return nc.values_load_multi_w_load_instructions(
                    emap[0:1, bass.ds(s, OCT)], engines=(mybir.EngineType.DVE,), min_val=0, max_val=E - 1,
                    skip_runtime_bounds_check_because="place() clamps them to 0..E-1")[1]

            def combine1(c, u):
                dve.wait_ge(gathered[u], (c - u) * (8 * QT * KSEL) + 16 * QT * KSEL)
                wait(dve, dve_out, c)
                gt = [gates[:, bass.ds(c * QT + t, 1), :].rearrange("p o k -> p (o k)") for t in range(QT)]
                for t in range(QT):
                    link(V.scalar_tensor_tensor(
                        yc[:, t, :], gath[:, u, 2 * t, :], gt[t][:, 0:1],
                        xhat2[:, bass.ds(c * QT + t, 1), :].rearrange("p o d -> p (o d)"), ALU.mult, ALU.add))
                me.wait()
                for t in range(QT):
                    link(V.scalar_tensor_tensor(yc[:, t, :], gath[:, u, 2 * t + 1, :], gt[t][:, 1:2],
                                                yc[:, t, :], ALU.mult, ALU.add))
                me.wait()
                for t in range(QT):
                    link(V.bn_stats(stc[:, t, :], yc[:, t, :]))
                settled()
                for t in range(QT):
                    m = V.bn_aggr(mvc[:, t, :], stc[:, t, :])
                    if t < QT - 1:
                        link(m)
                m.then_inc(dve_varc, 1)

            def combine2(c):
                dve.wait_ge(dve_varc, c + 1)
                newton(rc0[:], rc1[:], mvc[:, :, 1], act_rsc, c + 1)
                V.scalar_tensor_tensor(nmc[:], mvc[:, :, 0], -1.0, rc0[:], ALU.mult, ALU.mult).then_inc(dve_rstdc, 1)
                dve.wait_ge(act_x1c, (c + 1) * QT)
                link(V.tensor_tensor(uc, uc, beta[:].unsqueeze(1).broadcast_to([P, QT, H]), ALU.add))

            def combine3(c, u):
                dve.wait_ge(act_nc, (c + 1) * QT)
                link(V.tensor_tensor(yc, yc, gamma[:].unsqueeze(1).broadcast_to([P, QT, H]), ALU.mult))
                me.wait()
                wait(dve, o_out[u], (c - u) * 8)
                V.tensor_tensor(oc[:, u, :, :], yc, uc, ALU.add).then_inc(dve_out, 1)

            def oct(o, first=False, combine=None):
                ex = experts_of(o * OCT + 2)
                for r in range(OCT):
                    s = o * OCT + r
                    copy_weights(s + 2, r + 2, ex[r])
                    if not (first and r == 0):
                        if r % QT == 1:
                            wait(dve, y_out[r // QT], o * 16)
                        result(s - 1, (r - 1) % OCT)
                    if combine is not None:
                        c, u = combine
                        if r == 3:
                            combine1(c, u)
                        if r == 5:
                            combine2(c)
                        if r == 7:
                            combine3(c, u)

            ex = experts_of(0)
            dve.wait_ge(act_pack, 1)
            for r in range(2):
                copy_weights(r, r, ex[r])
            oct(0, first=True)
            with dve.Fori(1, NO) as o:
                oct(o)
            result(S_T - 1, OCT - 1)
            lead = NO - CQ
            oct(NO, first=True)
            with dve.Fori(NO + 1, NO + lead) as o:
                oct(o)
            for u in range(2):
                oct(NO + lead + u, combine=(u, u))
            with dve.Fori(1, CQ // 2) as c2:
                me.enter(c2, 1, 2 * LINKS_COMBINE)
                for u in range(2):
                    oct(c2 * 2 + (NO + lead + u), combine=(c2 * 2 + u, u))
            me.leave(CQ // 2 - 1)
            result(2 * S_T - 1, OCT - 1)
            with dve.Fori(CQ // 2, CQ) as c2:
                me.enter(c2, CQ // 2, 2 * LINKS_COMBINE)
                for u in range(2):
                    combine1(c2 * 2 + u, u)
                    combine2(c2 * 2 + u)
                    combine3(c2 * 2 + u, u)
            me.leave(CQ // 2)


_INS = ["x", "adj", "L0_gnn_w_rel1", "L0_gnn_w_root1", "L0_gnn_b1", "L0_gnn_w_rel2", "L0_gnn_w_root2",
        "L0_gnn_b2", "L0_ffn_gate_w", "L0_ffn_gate_b", "L0_ffn_w1", "L0_ffn_b1", "L0_ffn_w2", "L0_ffn_b2",
        "L0_ffn_gamma", "L0_ffn_beta"]
_OUTS = [((8, 1024, 128), "float32")]


def kernel(**inputs):
    import numpy as _np
    import concourse.bacc as _bacc
    from concourse import mybir as _mybir
    from concourse.bass_utils import run_bass_kernel_spmd as _run

    nc = _bacc.Bacc("TRN2", target_bir_lowering=False, num_devices=1)
    arrays, args = {}, []
    for name in _INS:
        a = _np.ascontiguousarray(inputs[name])
        arrays[f"in_{name}"] = a
        args.append(nc.dram_tensor(f"in_{name}", a.shape, _mybir.dt.from_np(a.dtype), kind="ExternalInput").ap())
    for i, (shape, dtype) in enumerate(_OUTS):
        dt = _mybir.dt.from_np(_np.dtype(dtype))
        args.append(nc.dram_tensor(f"out_{i}", shape, dt, kind="ExternalOutput").ap())
    gnn_moe_kernel(nc, *args)
    r = _run(nc, [arrays], core_ids=[0])
    return r.results[0]["out_0"]
```

```python
import concourse.bass as bass
from concourse import mybir
from contextlib import ExitStack


def gnn_moe_kernel(nc, x_d, adj_d, w_rel1_d, w_root1_d, b1g_d, w_rel2_d, w_root2_d, b2g_d,
                   gate_w_d, gate_b_d, w1_d, b1_d, w2_d, b2_d, gamma_d, beta_d, out_d):
    f32, f32r = mybir.dt.float32, mybir.dt.float32r
    bf16, i32, u32 = mybir.dt.bfloat16, mybir.dt.int32, mybir.dt.uint32
    ALU = mybir.AluOpType
    ACT = mybir.ActivationFunctionType
    AX = mybir.AxisListType

    NB, N, H = x_d.shape
    E, _, F = w1_d.shape
    P = 128
    T = N // P
    NT = NB * T
    KSEL = 2
    FH = F // P
    EPS = 1e-5
    GROUPS = [NB // 2, NB // 4, NB // 4]
    NG = len(GROUPS)
    B0 = [sum(GROUPS[:g]) for g in range(NG + 1)]
    OCT = 8
    NO = [-(-(n * T * KSEL + E - 1) // OCT) for n in GROUPS]
    O0 = [sum(NO[:g]) for g in range(NG + 1)]
    MAX_TILES = max(NO) * OCT
    QT = 4
    PAIRS = T // 2
    CQ = NT // QT
    LEAD = 2
    C0 = O0[1] + LEAD
    CT = O0[NG] - C0
    W2C, B1C, B2C = F, F + FH * H, F + FH * H + FH
    PACK = F + FH * H + FH + H
    PW = N // PAIRS
    AGW = 2 * H + 2

    x_v = x_d.rearrange("b (t p) d -> p (b t) d", p=P)
    out_v = out_d.rearrange("b (t p) d -> p (b t) d", p=P)
    adj_v = adj_d.rearrange("b (i p) j -> b p i j", p=P)
    SLOTS = [n * OCT * P for n in NO]
    xs_d = [nc.dram_tensor(f"expert_inputs_{g}", (SLOTS[g], H), f32).ap() for g in range(NG)]
    y_d = [nc.dram_tensor(f"expert_outputs_{g}", (SLOTS[g], H), f32).ap() for g in range(NG)]

    ctx = ExitStack()
    with ctx:
        def sb(name, shape, dt=f32):
            return ctx.enter_context(nc.sbuf_tensor(name, shape, dt))

        def pb(name, shape, dt=f32):
            return ctx.enter_context(nc.psum_tensor(name, shape, dt))

        def sem(name):
            return ctx.enter_context(nc.semaphore(name))

        xhat2 = sb("xhat2", [P, NT, H])
        mean2 = sb("mean2", [P, NT])
        std2 = sb("std2", [P, NT])
        gates = sb("gates", [P, NT, KSEL])
        pos = sb("pos", [P, NB, KSEL, T], i32)
        emap = sb("emap", [1, (O0[NG] + 1) * OCT], i32)
        ident = sb("ident", [P, P])
        gamma = sb("gamma", [P, H])
        beta = sb("beta", [P, H])
        b1c = sb("b1c", [P, E, FH])
        xb = sb("xb", [P, T, H])
        xh1 = sb("xh1", [P, T, H])
        xT = sb("xT", [P, N])
        h1 = sb("h1", [P, T, H])
        hT = sb("hT", [P, N])
        x1b = sb("x1b", [P, T, H])
        xn2 = sb("xn2", [P, T, H])
        yT = sb("yT", [P, N])
        zp = [sb(f"zp{c}", [P, T, AGW], f32r) for c in (1, 2)]
        hs = sb("hs", [P, 2, 2, H])
        sm = sb("sm", [P, 2, 2, H])
        vv = sb("vv", [P, 2, 2, H])
        ee = sb("ee", [P, 2, 2, H])
        mm_ = sb("mm_", [P, 2, 2, H])
        deg = sb("deg", [P, T, 1])
        rdeg = [sb(f"rdeg{k}", [P, T, 1]) for k in range(2)]
        wroot = [sb(f"wroot{c}", [P, H]) for c in (1, 2)]
        wrel = [sb(f"wrel{c}", [P, 2, H]) for c in (1, 2)]
        brow = [sb(f"brow{c}", [P, H]) for c in (1, 2)]
        biasf = sb("biasf", [P, 2, H])
        bhl = sb("bhl", [2, 2, H], f32r)
        ones2 = sb("ones2", [2, P], f32r)
        onez = sb("onez", [P, 2])
        b1rows = sb("b1rows", [E * FH, P])
        bhi = sb("bhi", [2, 2, H], f32r)
        blo = sb("blo", [2, 2, H])
        ones1 = sb("ones1", [2, P])
        zero = sb("zero", [P, 4 * P])
        epsb = sb("epsb", [P, 1])
        neg1 = sb("neg1", [P, 1])
        st = sb("st", [P, 2, T, 6])
        mv = sb("mv", [P, 2, T, 2])
        lnv = sb("lnv", [P, 2, T])
        rstd = sb("rstd", [P, 2, T])
        nwt = sb("nwt", [P, 2, T])
        nmr = sb("nmr", [P, 2, T])
        gate_w = sb("gate_w", [P, E])
        gate_b = sb("gate_b", [P, E])
        logit = sb("logit", [P, T, E])
        top = sb("top", [P, T, 8])
        topi = sb("topi", [P, T, 8], u32)
        sel_e = sb("sel_e", [P, KSEL, T])
        iota_e = sb("iota_e", [P, E])
        iota_s = sb("iota_s", [1, MAX_TILES])
        m12 = sb("m12", [P, NB, KSEL, T, E], bf16)
        m1 = sb("m1", [P, T, E], bf16)
        carry = sb("carry", [P, E], bf16)
        carryf = sb("carryf", [P, E])
        msum = sb("msum", [P, E])
        tri = sb("tri", [P, P], bf16)
        onesb = sb("onesb", [P, P], bf16)
        rsel = sb("rsel", [P, KSEL, T, E])
        rank = sb("rank", [P, NB, KSEL, T])
        cnti = sb("cnti", [P, E], i32)
        cntt = sb("cntt", [P, E], i32)
        ntl = sb("ntl", [P, E])
        incl = sb("incl", [P, E])
        base = sb("base", [P, E])
        zer16 = sb("zer16", [P, E])
        past = sb("past", [1, MAX_TILES, E], bf16)
        emf = sb("emf", [1, MAX_TILES])
        gq = sb("gq", [P, NT])
        gp = sb("gp", [P, NT])
        with ExitStack() as graph_phase:
            mask = [graph_phase.enter_context(nc.sbuf_tensor("mask_even", [P, T, T, P], f32r)), None]
            adj_st = graph_phase.enter_context(nc.sbuf_tensor("adj_st", [P, 2, T, PW], i32))
            mask[1] = graph_phase.enter_context(nc.sbuf_tensor("mask_odd", [P, T, T, P], f32r))
        pack = sb("pack", [P, E, PACK])
        xs = sb("xs", [P, 2, QT, H])
        xsT = sb("xsT", [P, 2, QT * P])
        wc = sb("wc", [P, OCT, PACK])
        ysb = sb("ysb", [P, 2, QT, H])
        gath = sb("gath", [P, 2, QT * KSEL, H])
        hid = sb("hid", [P, 4, FH, P])
        idxg = sb("idxg", [P, 2, KSEL, QT], i32)
        stc = sb("stc", [P, QT, 6])
        mvc = sb("mvc", [P, QT, 2])
        lnc = sb("lnc", [P, QT])
        rc0 = sb("rc0", [P, QT])
        rc1 = sb("rc1", [P, QT])
        nmc = sb("nmc", [P, QT])
        yc = xh1[:, 0:QT, :]
        uc = xh1[:, QT:2 * QT, :]
        oc = h1[:, :, :].rearrange("p (u t) d -> p u t d", u=2)

        AG = pb("AG", [P, 4, 512])
        TR = pb("TR", [P, 3, 512])
        GP = pb("GP", [P, 512])
        YB = [TR[:, 2, :], GP[:, :]]

        w_in = sem("w_in")
        pack_in = sem("pack_in")
        x_in = sem("x_in")
        xb_in = sem("xb_in")
        adj_in = [sem(f"adj_in{u}") for u in range(2)]
        xs_zeroed = sem("xs_zeroed")
        scattered = [sem(f"scattered{g}") for g in range(NG)]
        xs_in = [sem(f"xs_in{u}") for u in range(2)]
        y_out = [sem(f"y_out{u}") for u in range(2)]
        gathered = [sem(f"gathered{u}") for u in range(2)]
        o_out = [sem(f"o_out{u}") for u in range(2)]
        pool_const = sem("pool_const")
        pool_idx = sem("pool_idx")
        dve_const = sem("dve_const")
        dve_self = sem("dve_self")
        pe_b1 = sem("pe_b1")
        act_b1, act_pack = sem("act_b1"), sem("act_pack")
        pe_xT, pe_hT, pe_yT = sem("pe_xT"), sem("pe_hT"), sem("pe_yT")
        act_xT, act_hT, act_yT = sem("act_xT"), sem("act_hT"), sem("act_yT")
        pe_z, act_zhi, dve_zlo = sem("pe_z"), sem("act_zhi"), sem("dve_zlo")
        pe_ag, act_aghi, dve_v = sem("pe_ag"), sem("act_aghi"), sem("dve_v")
        act_e, dve_h = sem("act_e"), sem("dve_h")
        dve_mask, pool_mask = sem("dve_mask"), sem("pool_mask")
        dve_var, act_ln, act_rs = sem("dve_var"), sem("act_ln"), sem("act_rs")
        dve_rstd = sem("dve_rstd")
        pool_xh1, act_xh2 = sem("pool_xh1"), sem("act_xh2")
        xh2_kept = sem("xh2_kept")
        pe_gate, dve_m1, pe_rank, dve_rank = sem("pe_gate"), sem("dve_m1"), sem("pe_rank"), sem("dve_rank")
        dve_carry = sem("dve_carry")
        pe_cnt, dve_cnt, dve_pos = sem("pe_cnt"), sem("dve_cnt"), sem("dve_pos")
        dve_reset = sem("dve_reset")
        dve_gd, act_gp = sem("dve_gd"), sem("act_gp")
        pe_xsT, act_xsT = sem("pe_xsT"), sem("act_xsT")
        dve_wc, pe_up, act_h = sem("dve_wc"), sem("pe_up"), sem("act_h")
        pe_y, dve_y = sem("pe_y"), sem("dve_y")
        dve_out = sem("dve_out")
        passed, passed_pool = sem("passed"), sem("passed_pool")
        dve_gath = sem("dve_gath")
        dve_varc, act_lnc, act_rsc = sem("dve_varc"), sem("act_lnc"), sem("act_rsc")
        dve_rstdc, act_x1c, act_nc = sem("dve_rstdc"), sem("act_x1c"), sem("act_nc")
        act_gated = sem("act_gated")

        def wait(eng, s, v):
            if isinstance(v, int) and v <= 0:
                return
            eng.wait_ge(s, v)

        def pair_no(c, i, p):
            if isinstance(i, int) and i == 0:
                return p
            if isinstance(i, int) and i == NB:
                return 2 * PAIRS * NB - PAIRS + p
            return i * (2 * PAIRS) - PAIRS * (1 - c) + p

        def z_no(c, b, u):
            if c == 0:
                return u if isinstance(b, int) and b == 0 else b * 4 - 2 + u
            return NB * 4 - 2 + u if isinstance(b, int) and b == NB - 1 else b * 4 + 4 + u

        def stats_no(k, b):
            return b + 1 if k == 0 else b + 4

        def kinds(at):
            return slice(0 if at < NB - 1 else 1, 2 if at > 1 else 1)

        block = ctx.enter_context(nc.Block())

        LAG = 2
        AHEAD = 3
        ACT_NORMS = 2
        N_SMALL = 11
        N_DCONST = 10
        LINKS_STEPS = 160
        LINKS_COMBINE = 16
        N_CONST = 8
        CLEARED = zero.shape[1] // H * P
        ZEROINGS = sum(SLOTS) // CLEARED

        @block.sync
        def _(sp):
            sp.dma_start(xhat2[:, 0:T, :], x_v[:, 0:T, :]).then_inc(x_in, 16)

            def adj_load(b, p):
                wait(sp, dve_mask, b * PAIRS + p - 1)
                wait(sp, pool_mask, b * PAIRS + p - 1)
                src = adj_v[bass.ds(b, 1), :, :, p * PW:(p + 1) * PW]
                sp.dma_start(adj_st[:, p % 2, :, :], src.rearrange("o p i j -> (o p) i j"))\
                    .then_inc(adj_in[p % 2], 16)

            def keep(b):
                sp.wait_ge(act_xh2, (b + 1) * T)
                sp.dma_start(xhat2[:, bass.ds(b * T, T), :].rearrange("p t d -> p (t d)"),
                             xn2[:].rearrange("p t d -> p (t d)")).then_inc(xh2_kept, 16)

            def clear(g, n, parts):
                zs_v = xs_d[g].rearrange("(z p r) d -> z p (r d)", p=P, r=CLEARED // P)
                per = SLOTS[g] // CLEARED // parts
                for z in range(per):
                    dst = zs_v[bass.ds(n * per + z, 1)]
                    sp.dma_start(dst.rearrange("o p c -> (o p) c"), zero[:]).then_inc(xs_zeroed, 16)

            def step_loads(b, cleared, kept=True):
                load_x(b)
                copy_x(b)
                for p in range(2):
                    adj_load(b, p)
                for c in cleared:
                    clear(*c)
                if kept:
                    keep(b - 3)
                for p in range(2, PAIRS):
                    adj_load(b, p)

            def load_x(b):
                sp.wait_ge(x_in, b * 16)
                sp.dma_start(xhat2[:, bass.ds(b * T, T), :], x_v[:, bass.ds(b * T, T), :]).then_inc(x_in, 16)

            def copy_x(b):
                sp.wait_ge(x_in, (b + 1) * 16)
                sp.wait_ge(pool_xh1, b * T)
                sp.dma_start(xb[:].rearrange("p t d -> p (t d)"),
                             xhat2[:, bass.ds(b * T, T), :].rearrange("p t d -> p (t d)")).then_inc(xb_in, 16)

            sp.dma_start(xb[:], x_v[:, 0:T, :]).then_inc(xb_in, 16)
            for p in range(PAIRS):
                adj_load(0, p)
            sp.wait_ge(pool_const, N_CONST)
            for b in (1, 2):
                step_loads(b, [(0, b - 1, B0[1])], kept=False)
            with sp.Fori(3, B0[1] + 1) as b:
                step_loads(b, [(0, b - 1, B0[1])])
            with sp.Fori(B0[1] + 1, NB) as b:
                step_loads(b, [(g, b - (B0[1] + 1), NB - 1 - B0[1]) for g in range(1, NG)])
            keep(NB - 3)
            sp.wait_ge(pe_ag, pair_no(1, NB - 1, PAIRS))
            sp.wait_ge(dve_mask, NB * PAIRS)
            sp.wait_ge(pool_mask, NB * PAIRS)
            sp.dma_start(pack[:, :, 0:F], w1_d.rearrange("e h f -> h e f")).then_inc(pack_in, 16)
            w2_v = w2_d.rearrange("e (c p) h -> c p e h", p=P)
            for c in range(FH):
                sp.dma_start(pack[:, :, W2C + c * H:W2C + (c + 1) * H], w2_v[c]).then_inc(pack_in, 16)
            sp.dma_start(pack[:, :, B2C:B2C + H], b2_d.partition_broadcast(P)).then_inc(pack_in, 16)
            keep(NB - 2)
            keep(NB - 1)

            def xs_load(q, g, u):
                wait(sp, pe_xsT, q - 1)
                src = xs_d[g].rearrange("(q t p) d -> q p t d", t=QT, p=P)[bass.ds(q - 2 * O0[g], 1)]
                sp.dma_start(xs[:, u, :, :], src.rearrange("o p t d -> (o p) t d")).then_inc(xs_in[u], 16)

            def y_store(q, g, u):
                sp.wait_ge(dve_y, (q + 1) * QT)
                dst = y_d[g].rearrange("(q t p) d -> q p t d", t=QT, p=P)[bass.ds(q - 2 * O0[g], 1)]
                sp.dma_start(dst.rearrange("o p t d -> (o p) t d"), ysb[:, u, :, :]).then_inc(y_out[u], 16)

            def out_store(c, u):
                sp.wait_ge(dve_out, c + 1)
                dst = out_v[:, bass.ds(c * QT, QT), :]
                sp.dma_start(dst, oc[:, u, :, :]).then_inc(o_out[u], 16)

            def oct_io(o, g, u=None, following=None):
                g3, g4 = following or (g, g)
                if g3 < NG:
                    xs_load(2 * o + 3, g3, 1)
                y_store(2 * o, g, 0)
                if g4 < NG:
                    xs_load(2 * o + 4, g4, 0)
                if u is not None:
                    out_store(o - C0, u)
                y_store(2 * o + 1, g, 1)

            def arrived(g):
                sp.wait_ge(scattered[g], 16 * KSEL * T * GROUPS[g])

            sp.wait_ge(pe_ag, 2 * NB * PAIRS)
            arrived(0)
            for q in range(3):
                xs_load(q, 0, q % 2)
            for g in range(NG):
                start, end = O0[g], O0[g + 1] - 2
                if start < C0:
                    with sp.Fori(start, min(end, C0)) as o:
                        oct_io(o, g)
                if end > C0:
                    with sp.Fori(max(start, C0) // 2, end // 2) as h:
                        for u in range(2):
                            oct_io(h * 2 + u, g, u)
                if g + 1 < NG:
                    arrived(g + 1)
                for u in range(2):
                    oct_io(end + u, g, u if end >= C0 else None, following=(g + u, g + 1))
            with sp.Fori(CT // 2, CQ // 2) as c2:
                for u in range(2):
                    out_store(c2 * 2 + u, u)
            for u in range(2):
                sp.wait_ge(o_out[u], 16 * CQ // 2)
                sp.wait_ge(y_out[u], 16 * O0[NG])

        @block.gpsimd
        def _(pool):
            nc.gpsimd.memset(ident[:], 0.0).then_inc(pool_const, 1)
            nc.gpsimd.memset(tri[:], 1.0).then_inc(pool_const, 1)
            nc.gpsimd.memset(onesb[:], 1.0).then_inc(pool_const, 1)
            nc.gpsimd.memset(zero[:], 0.0).then_inc(pool_const, 1)
            nc.gpsimd.iota(iota_e[:], [[1, E]], base=0, channel_multiplier=0,
                           allow_small_or_imprecise_dtypes=True).then_inc(pool_const, 1)
            nc.gpsimd.iota(iota_s[:], [[1, MAX_TILES]], base=0, channel_multiplier=0,
                           allow_small_or_imprecise_dtypes=True).then_inc(pool_const, 1)
            pool.wait_ge(pool_const, 6)
            nc.gpsimd.affine_select(out=ident[:], in_=ident[:], compare_op=ALU.not_equal, fill=1.0,
                                    base=0, pattern=[[-1, P]], channel_multiplier=1).then_inc(pool_const, 1)
            nc.gpsimd.affine_select(out=tri[:], in_=tri[:], compare_op=ALU.is_gt, fill=0.0,
                                    base=0, pattern=[[1, P]], channel_multiplier=-1).then_inc(pool_const, 1)

            def mask_odd(b, p, parity):
                pool.wait_ge(adj_in[p % 2], b * 32 + (p // 2 + 1) * 16)
                if not isinstance(b, int):
                    pool.wait_ge(pe_ag, pair_no(1, b - 1, p) + 1)
                    pool.sem_inc(passed_pool, 1)
                nc.gpsimd.tensor_scalar(mask[parity][:, 2 * p + 1, :, :], adj_st[:, p % 2, :, P:2 * P],
                                        1, None, ALU.is_equal).then_inc(pool_mask, 1)

            def layernorm1(b):
                pool.wait_ge(dve_rstd, stats_no(0, b))
                wait(pool, pe_xT, b * 2)
                pool.wait_ge(xb_in, b * 16 + 16)
                pool.sem_inc(passed_pool, 1)
                for t in range(T):
                    nc.gpsimd.tensor_scalar(xh1[:, t, :], xb[:, t, :],
                                            rstd[:, 0, t:t + 1], nmr[:, 0, t:t + 1], ALU.mult, ALU.add)\
                        .then_inc(pool_xh1, 1)

            for b in range(2):
                if b > 0:
                    layernorm1(b)
                for p in range(PAIRS):
                    mask_odd(b, p, b)
                    if b == 0 and p == 0:
                        layernorm1(0)
            with pool.Fori(1, NB // 2) as k:
                for parity in range(2):
                    layernorm1(k * 2 + parity)
                    for p in range(PAIRS):
                        mask_odd(k * 2 + parity, p, parity)

            for g in range(NG):
                pool.wait_ge(xh2_kept, 16 * B0[g + 1])
                if g == 0:
                    pool.wait_ge(xs_zeroed, 16 * ZEROINGS)
                for b in range(B0[g], B0[g + 1]):
                    pool.wait_ge(dve_pos, b + 1)
                    for t in range(T):
                        for k in range(KSEL):
                            pool.indirect_dma_start(
                                xs_d[g][:, :], bass.IndirectOffsetOnAxis(ap=pos[:, b, k, t:t + 1], axis=0),
                                xhat2[:, b * T + t, :], None).then_inc(scattered[g], 16)
            for g in range(NG):
                for u in range(2):
                    pool.wait_ge(y_out[u], 16 * O0[g + 1])
                def gather_batch(n):
                    first = isinstance(n, int) and n == 0
                    for u in range(2):
                        if not first:
                            pool.wait_ge(gathered[u], n * (16 * QT * KSEL))
                            pool.wait_ge(dve_gath, n * 2 - 1 + u)
                        nc.gpsimd.tensor_copy(
                            idxg[:, u, :, :],
                            pos[:, bass.ds(n, 1), :, u * QT:(u + 1) * QT]
                            .rearrange("p o k t -> p (o k) t")).then_inc(pool_idx, 1)
                        pool.wait_ge(pool_idx, n * 2 + u + 1)
                        pool.sem_inc(passed_pool, 1)
                        for t in range(QT):
                            for k in range(KSEL):
                                pool.indirect_dma_start(
                                    gath[:, u, t * KSEL + k, :], None, y_d[g][:, :],
                                    bass.IndirectOffsetOnAxis(ap=idxg[:, u, k, t:t + 1], axis=0)
                                ).then_inc(gathered[u], 16)

                if g == 0:
                    gather_batch(0)
                with pool.Fori(max(1, B0[g]), B0[g + 1]) as n:
                    gather_batch(n)

        @block.tensor
        def _(pe):
            def transposes(src, u, bank, done):
                for t in range(QT):
                    m = nc.tensor.transpose(TR[:, bank, t * P:(t + 1) * P], src[:, u * QT + t, :], ident[:])
                m.then_inc(done, 1)

            def project(c, u, srcT, bank):
                for t in range(QT):
                    n = (u * QT + t) * P
                    m = nc.tensor.matmul(TR[:, bank, t * H:(t + 1) * H], srcT[:, n:n + P],
                                         wrel[c][:, 1, :], start=True, stop=True)
                m.then_inc(pe_z, 1)

            def aggregate(c, i, p, srcT, parity):
                b = i - c
                if p == 0:
                    pe.wait_ge(dve_zlo, z_no(c, b, 1) + 1)
                if c == 0:
                    pe.wait_ge(dve_mask, b * PAIRS + p + 1)
                    pe.wait_ge(pool_mask, b * PAIRS + p + 1)
                wait(pe, dve_v, pair_no(c, i, p) - 1)
                width = AGW if c == 0 else 2 * H
                for j in (2 * p, 2 * p + 1):
                    o = AG[:, 2 * (p % 2) + j % 2, :]
                    for k in range(T):
                        nc.tensor.matmul(o[:, 0:width], mask[parity][:, j, k, :], zp[c][:, k, 0:width],
                                         start=(k == 0), stop=(k == T - 1))
                    nc.tensor.matmul(o[:, 260:260 + H], srcT[:, j * P:(j + 1) * P], wroot[c][:],
                                     start=True, stop=False)
                    m = nc.tensor.matmul(o[:, 260:260 + H], ones2[:], bhl[:, c, :],
                                         start=False, stop=True)
                m.then_inc(pe_ag, 1)

            def gate(b):
                pe.wait_ge(act_yT, b * 2 + 2)
                wait(pe, dve_rank, b)
                for t in range(T):
                    m = nc.tensor.matmul(GP[:, t * E:(t + 1) * E], yT[:, t * P:(t + 1) * P], gate_w[:],
                                         start=True, stop=True)
                m.then_inc(pe_gate, 1)

            def ranks(b, g):
                pe.wait_ge(dve_m1, b + 1)
                wait(pe, dve_carry, b)
                wait(pe, dve_reset, g)
                o = GP[:, T * E:2 * T * E].rearrange("p (t e) -> p t e", e=E)
                nc.tensor.matmul(o, tri[:], m1[:, :, :], start=True, stop=False)
                for t in range(T - 1):
                    nc.tensor.matmul(o[:, t + 1:T, :], onesb[:],
                                     m1[:, t:t + 1, :].broadcast_to([P, T - 1 - t, E]), start=False, stop=False)
                nc.tensor.matmul(o, onesb[:], carry[:].unsqueeze(1).broadcast_to([P, T, E]),
                                 start=False, stop=True).then_inc(pe_rank, 1)

            def counts(g):
                pe.wait_ge(dve_carry, B0[g + 1])
                pe.wait_ge(dve_rank, B0[g + 1])
                nc.tensor.matmul(GP[:, 2 * T * E:2 * T * E + E], onesb[:], carry[:],
                                 start=True, stop=True).then_inc(pe_cnt, 1)

            def transpose_y(b, u):
                pe.wait_ge(act_xh2, b * T + (u + 1) * QT)
                transposes(xn2, u, 1 + u, pe_yT)

            def step(i, parity):
                at = i if isinstance(i, int) else 3
                conv1, conv2 = at < NB, at > 0
                for p in range(PAIRS):
                    if conv1:
                        aggregate(0, i, p, xT, parity)
                    if conv2 and p < 2:
                        pe.wait_ge(act_hT, (i - 1) * 2 + p + 1)
                        if p == 0:
                            if at > 2:
                                pe.wait_ge(act_yT, (i - 3) * 2 + 2)
                            if at < NB:
                                pe.wait_ge(dve_zlo, z_no(0, i, 0) + 1)
                        project(1, p, hT, 2 if p == 0 else 0)
                for p in range(PAIRS):
                    if conv2:
                        aggregate(1, i, p, hT, 1 - parity)
                    if p == 0 and at < NB - 1:
                        if conv2:
                            pe.wait_ge(dve_zlo, z_no(1, i - 1, 1) + 1)
                        else:
                            pe.wait_ge(dve_zlo, z_no(0, 0, 1) + 1)
                        for u in range(2):
                            if u == 1 and conv2:
                                pe.wait_ge(act_hT, (i - 1) * 2 + 2)
                            pe.wait_ge(pool_xh1, (i + 1) * T + (u + 1) * QT)
                            transposes(xh1, u, u, pe_xT)
                    if p == 1 and at > 2:
                        ranks(i - 3, 0 if at < B0[1] + 3 else 1)
                    if p in (1, 2) and at < NB - 1:
                        pe.wait_ge(act_xT, (i + 1) * 2 + p)
                        if p == 1 and conv2:
                            pe.wait_ge(dve_zlo, z_no(1, i - 1, 0) + 1)
                        project(0, p - 1, xT, 2 if p == 1 else 0)
                    if p == 2 and at > 1:
                        if at < NB - 1:
                            pe.wait_ge(act_xT, (i + 1) * 2 + 2)
                        else:
                            pe.wait_ge(act_hT, i * 2)
                        transpose_y(i - 2, 0)
                        pe.wait_ge(dve_zlo, (z_no(0, i + 1, 0) if at < NB - 1 else z_no(1, i - 1, 0)) + 1)
                        transpose_y(i - 2, 1)
                if conv1:
                    for u in range(2):
                        pe.wait_ge(dve_h, pair_no(0, i, 2 * u + 1) + 1)
                        if u == 0:
                            pe.wait_ge(dve_zlo, (z_no(0, i + 1, 1) if at < NB - 1 else z_no(1, i - 1, 1)) + 1)
                        elif at > 1:
                            pe.wait_ge(act_yT, (i - 2) * 2 + 1)
                        elif at == 0 or at == 1:
                            pe.wait_ge(act_xT, (i + 1) * 2 + 2)
                        transposes(h1, u, u, pe_hT)
                if at > 1:
                    gate(i - 2)

            pe.wait_ge(pool_const, N_CONST)
            pe.wait_ge(w_in, 16 * N_SMALL)
            for c in range(2):
                nc.tensor.matmul(GP[:, c * H:(c + 1) * H], zero[:, 0:P], wrel[c][:, 0, :],
                                 start=True, stop=True)
            nc.tensor.transpose(GP[:, 2 * H:2 * H + E * FH], b1rows[:], ident[0:E * FH, 0:E * FH]).then_inc(pe_b1, 1)
            for u in range(2):
                pe.wait_ge(pool_xh1, (u + 1) * QT)
                transposes(xh1, u, u, pe_xT)
            for u in range(2):
                pe.wait_ge(act_xT, u + 1)
                project(0, u, xT, 2 if u == 0 else 0)
            pe.wait_ge(dve_const, N_DCONST)
            for i in range(3):
                step(i, i % 2)
            with pe.Fori(1, (NB - 2) // 2) as k:
                step(k * 2 + 1, 1)
                step(k * 2 + 2, 0)
            counts(0)
            for i in (NB - 1, NB):
                step(i, i % 2)
            counts(1)
            ranks(NB - 2, 2)
            pe.wait_ge(dve_zlo, NB * 4)
            pe.wait_ge(act_yT, (NB - 1) * 2)
            for u in range(2):
                transpose_y(NB - 1, u)
            gate(NB - 1)
            ranks(NB - 1, 2)
            counts(2)

            def slot_transposes(q, u):
                wait(pe, act_xsT, q - 1)
                pe.wait_ge(xs_in[u], (q - u) * 8 + 16)
                for t in range(QT):
                    m = nc.tensor.transpose(TR[:, u, t * P:(t + 1) * P], xs[:, u, t, :], ident[:])
                m.then_inc(pe_xsT, 1)

            def down(s, r):
                pe.wait_ge(act_h, s + 1)
                wait(pe, dve_y, s - 1)
                for half in range(FH):
                    m = nc.tensor.matmul(YB[r % 2][:, 0:H], hid[:, r % 4, half, :],
                                         wc[:, r, W2C + half * H:W2C + (half + 1) * H],
                                         start=(half == 0), stop=(half == FH - 1))
                m.then_inc(pe_y, 1)

            def oct(o, first=False, last=False):
                for r in range(OCT):
                    u, t = r // QT, r % QT
                    if t == 0:
                        pe.wait_ge(act_xsT, o * 2 + u + 1)
                    s = o * OCT + r
                    pe.wait_ge(dve_wc, s + 1)
                    wait(pe, act_h, s - 3)
                    for half in range(FH):
                        m = nc.tensor.matmul(AG[:, r % 4, half * P:(half + 1) * P],
                                             wc[:, r, half * P:(half + 1) * P],
                                             xsT[:, u, t * P:(t + 1) * P], start=True, stop=True)
                    m.then_inc(pe_up, 1)
                    if not (first and r < LAG):
                        down(s - LAG, (r - LAG) % OCT)
                    if r == 1:
                        slot_transposes(o * 2 + 1, 1)
                    if r == 5 and not last:
                        slot_transposes(o * 2 + 2, 0)

            pe.wait_ge(dve_v, 2 * NB * PAIRS)
            pe.wait_ge(act_yT, NB * 2)
            pe.wait_ge(dve_cnt, NG)
            slot_transposes(0, 0)
            oct(0, first=True)
            with pe.Fori(1, O0[NG] - 1) as o:
                oct(o)
            oct(O0[NG] - 1, last=True)
            for r in range(OCT - LAG, OCT):
                down((O0[NG] - 1) * OCT + r, r)

        @block.scalar
        def _(act):
            small = [(wroot[0][:], w_root1_d), (wroot[1][:], w_root2_d),
                     (wrel[0][:], w_rel1_d.rearrange("r d e -> d r e")),
                     (wrel[1][:], w_rel2_d.rearrange("r d e -> d r e")),
                     (brow[0][:], b1g_d.partition_broadcast(P)), (brow[1][:], b2g_d.partition_broadcast(P)),
                     (gate_w[:], gate_w_d), (gate_b[:], gate_b_d.partition_broadcast(P)),
                     (gamma[:], gamma_d.partition_broadcast(P)), (beta[:], beta_d.partition_broadcast(P)),
                     (b1rows[:], b1_d.rearrange("e (c p) -> (e c) p", p=P))]
            assert len(small) == N_SMALL
            for dst, src in small:
                act.dma_start(dst, src).then_inc(w_in, 16)
            act.preload_act_table_set("natural_log_exp_and_others")

            def rsqrt(var, ready, n, ln_out, out, s_ln, s_out):
                act.wait_ge(ready, n)
                nc.scalar.activation(ln_out, var, ACT.Ln, bias=epsb[:, 0:1]).then_inc(s_ln, 1)
                act.wait_ge(s_ln, n)
                nc.scalar.activation(out, ln_out, ACT.Exp, scale=-0.5).then_inc(s_out, 1)

            def ln_rsqrt(n, ks):
                rsqrt(mv[:, ks, :, 1], dve_var, n, lnv[:, ks], rstd[:, ks], act_ln, act_rs)

            def norm(k, b, u, dst, done, src):
                act.wait_ge(dve_rstd, stats_no(k, b))
                for t in range(u * QT, (u + 1) * QT):
                    nc.scalar.activation(dst[:, t, :], src(t), ACT.Identity, scale=rstd[:, k, t:t + 1],
                                         bias=nmr[:, k, t:t + 1]).then_inc(done, 1)

            def x_tile(b):
                return lambda t: xhat2[:, bass.ds(b * T + t, 1), :].rearrange("p o d -> p (o d)")

            def layernorm2(b, u):
                wait(act, pe_yT, b * 2)
                wait(act, xh2_kept, b * 16)
                norm(1, b, u, xn2, act_xh2, lambda t: x1b[:, t, :])

            def evac(dst, u, bank, ready, r, done, less_one=False):
                act.wait_ge(ready, r)
                o, i = dst[:, u * 512:(u + 1) * 512], TR[:, bank, :]
                if less_one:
                    m = nc.scalar.activation(o, i, ACT.Identity, bias=neg1[:, 0:1])
                else:
                    m = nc.scalar.activation(o, i, ACT.Copy)
                m.then_inc(done, 1)

            def high(c, b, u):
                act.wait_ge(pe_z, z_no(c, b, u) + 1)
                nc.scalar.activation(zp[c][:, u * QT:(u + 1) * QT, 0:H],
                                     TR[:, 2 if u == 0 else 0, :].rearrange("p (t d) -> p t d", t=QT), ACT.Copy)\
                    .then_inc(act_zhi, 1)

            def high_sum(n, r):
                act.wait_ge(pe_ag, n + 1)
                wait(act, dve_v, n - 1)
                nc.scalar.activation(hs[:, r, :, :], AG[:, 2 * r:2 * r + 2, 0:H], ACT.Copy).then_inc(act_aghi, 1)

            def exps(n, r):
                act.wait_ge(dve_v, n + 1)
                wait(act, dve_h, n - 1)
                nc.scalar.activation(ee[:, r, :, :], vv[:, r, :, :], ACT.Exp, bias=neg1[:, 0:1]).then_inc(act_e, 1)

            def y_evac(b, u):
                wait(act, pe_gate, b)
                evac(yT, u, 1 + u, pe_yT, b * 2 + u + 1, act_yT)

            def step(i):
                at = i if isinstance(i, int) else 3
                conv1, conv2, more = at < NB, at > 0, at < NB - 1
                for p in range(PAIRS):
                    if conv1:
                        high_sum(pair_no(0, i, p), p % 2)
                    if p == 0 and not conv1:
                        for u in range(2):
                            high(1, i - 1, u)
                    if p == 0:
                        ln_rsqrt(i + 2, kinds(at))
                    if p < 2 and conv1 and conv2:
                        high(1, i - 1, p)
                    if conv1:
                        exps(pair_no(0, i, p), p % 2)
                    if p == 3 and at > 1:
                        layernorm2(i - 2, 0)
                for p in range(PAIRS):
                    if conv2:
                        high_sum(pair_no(1, i, p), p % 2)
                    if p == 0 and more:
                        for u in range(2):
                            evac(xT, u, u, pe_xT, (i + 1) * 2 + u + 1, act_xT)
                    if p in (1, 2) and more:
                        high(0, i + 1, p - 1)
                    if conv2:
                        exps(pair_no(1, i, p), p % 2)
                    if p == 0 and at > 1:
                        layernorm2(i - 2, 1)
                    if p == 2 and at > 1:
                        for u in range(2):
                            y_evac(i - 2, u)
                if conv1:
                    for u in range(2):
                        evac(hT, u, u, pe_hT, i * 2 + u + 1, act_hT, True)

            act.wait_ge(dve_const, 4)
            ln_rsqrt(1, kinds(0))
            act.wait_ge(pe_b1, 1)
            nc.scalar.activation(b1c[:], GP[:, 2 * H:2 * H + E * FH].rearrange("p (e c) -> p e c", c=FH),
                                 ACT.Copy).then_inc(act_b1, 1)
            for u in range(2):
                evac(xT, u, u, pe_xT, u + 1, act_xT)
            for u in range(2):
                high(0, 0, u)
            for i in range(3):
                step(i)
            with act.Fori(1, (NB - 2) // 2) as k:
                step(k * 2 + 1)
                step(k * 2 + 2)
            for i in (NB - 1, NB):
                step(i)
            ln_rsqrt(NB + 3, kinds(NB))
            for u in range(2):
                layernorm2(NB - 1, u)
            for u in range(2):
                y_evac(NB - 1, u)
            act.wait_ge(pack_in, 16 * (2 + FH))
            nc.scalar.activation(pack[:, :, B1C:B1C + FH], b1c[:], ACT.Copy).then_inc(act_pack, 1)

            def slot_evac(q, u):
                act.wait_ge(pe_xsT, q + 1)
                wait(act, pe_up, (q - 1) * QT)
                nc.scalar.activation(xsT[:, u, :], TR[:, u, :], ACT.Copy).then_inc(act_xsT, 1)

            def gated(c, u):
                act.wait_ge(gathered[u], (c - u) * (8 * QT * KSEL) + 16 * QT * KSEL)
                for n in range(QT * KSEL):
                    t, k = n // KSEL, n % KSEL
                    gate = gates[:, bass.ds(c * QT + t, 1), k:k + 1].rearrange("p o k -> p (o k)")
                    m = nc.scalar.activation(gath[:, u, n, :], gath[:, u, n, :], ACT.Copy, scale=gate)
                m.then_inc(act_gated, 1)

            def combine(c):
                wait(act, dve_out, c)
                for t in range(QT):
                    nc.scalar.activation(uc[:, t, :], xhat2[:, bass.ds(c * QT + t, 1), :].rearrange("p o d -> p (o d)"),
                                         ACT.Identity, scale=std2[:, bass.ds(c * QT + t, 1)],
                                         bias=mean2[:, bass.ds(c * QT + t, 1)]).then_inc(act_x1c, 1)
                rsqrt(mvc[:, :, 1], dve_varc, c + 1, lnc[:], rc0[:], act_lnc, act_rsc)

            def combine_norm(c):
                act.wait_ge(dve_rstdc, c + 1)
                for t in range(ACT_NORMS):
                    m = nc.scalar.activation(yc[:, t, :], yc[:, t, :], ACT.Identity, scale=rc0[:, t:t + 1],
                                             bias=nmc[:, t:t + 1])
                m.then_inc(act_nc, 1)

            def oct(o, last=False, quad=None):
                for r in range(OCT):
                    s = o * OCT + r
                    act.wait_ge(pe_up, s + 1)
                    wait(act, pe_y, s - 3)
                    for half in range(FH):
                        m = nc.scalar.activation(hid[:, r % 4, half, :], AG[:, r % 4, half * P:(half + 1) * P],
                                                 ACT.Relu, bias=wc[:, r, B1C + half:B1C + half + 1])
                    m.then_inc(act_h, 1)
                    if r == 1:
                        slot_evac(o * 2 + 1, 1)
                    if r == 5 and not last:
                        slot_evac(o * 2 + 2, 0)
                    if quad is not None and r == 0:
                        gated(*quad)
                    if quad is not None and r == 3:
                        combine(quad[0])
                    if quad is not None and r == 6:
                        combine_norm(quad[0])

            slot_evac(0, 0)
            oct(0)
            act.wait_ge(dve_gd, 1)
            nc.scalar.activation(gp[:], gq[:], ACT.Exp).then_inc(act_gp, 1)
            with act.Fori(1, C0) as o:
                oct(o)
            for u in range(2):
                oct(C0 + u, quad=(u, u))
            with act.Fori(C0 // 2 + 1, O0[NG] // 2 - 1) as h:
                for u in range(2):
                    oct(h * 2 + u, quad=(h * 2 + (u - C0), u))
            for u in range(2):
                oct(O0[NG] - 2 + u, last=u == 1, quad=(O0[NG] - 2 + u - C0, u))
            with act.Fori(CT // 2, CQ // 2) as c2:
                for u in range(2):
                    gated(c2 * 2 + u, u)
                    combine(c2 * 2 + u)
                    combine_norm(c2 * 2 + u)

        @block.vector
        def _(dve):
            class Self:
                base, n = 0, 0

                def link(self, ins):
                    ins.then_inc(dve_self, 1)
                    self.n += 1
                    return self.n

                def wait(self, n=None):
                    dve.wait_ge(dve_self, self.base + (self.n if n is None else n))

                def enter(self, i, start, per):
                    self.base0, self.n0 = self.base + self.n, per
                    self.base, self.n = (i - start) * per + self.base0, 0

                def leave(self, times):
                    assert self.n == self.n0, (self.n, self.n0)
                    self.base, self.n = self.base0 + times * self.n0, 0

            me = Self()

            def settled():
                me.wait()
                dve.sem_inc(passed, 1)

            link = me.link
            V = nc.vector

            V.memset(onez[:, 0:1], 1.0).then_inc(dve_const, 1)
            V.memset(onez[:, 1:2], 0.0).then_inc(dve_const, 1)
            V.memset(epsb[:], EPS).then_inc(dve_const, 1)
            V.memset(neg1[:], -1.0).then_inc(dve_const, 1)
            link(V.memset(ones1[:], 1.0))
            link(V.memset(zer16[:], 0.0))
            link(V.memset(carryf[:], 0.0))
            V.memset(carry[:], 0.0).then_inc(dve_const, 1)
            V.memset(emap[0:1, O0[NG] * OCT:], 0).then_inc(dve_const, 1)
            dve.wait_ge(dve_const, 6)
            me.wait()
            for c in range(2):
                V.tensor_copy(zp[c][:, :, 2 * H:AGW], onez[:].unsqueeze(1).broadcast_to([P, T, 2]))\
                    .then_inc(dve_const, 1)
            V.tensor_copy(ones2[:], ones1[:]).then_inc(dve_const, 1)

            def ln_stats(k, src, tiles=range(T)):
                for t in tiles:
                    link(V.bn_stats(st[:, k, t, :], src(t)))

            def ln_var(ks):
                settled()
                of = [(k, t) for k in range(2)[ks] for t in range(T)]
                for k, t in of:
                    m = V.bn_aggr(mv[:, k, t, :], st[:, k, t, :])
                    if (k, t) != of[-1]:
                        link(m)
                m.then_inc(dve_var, 1)

            def newton(r, s, var, ready, n):
                dve.wait_ge(ready, n)
                link(V.tensor_tensor(s, r, r, ALU.mult))
                me.wait()
                link(V.scalar_tensor_tensor(s, var, EPS, s, ALU.add, ALU.mult))
                me.wait()
                link(V.tensor_scalar(s, s, -0.5, 1.5, ALU.mult, ALU.add))
                me.wait()
                link(V.tensor_tensor(r, r, s, ALU.mult))
                me.wait()

            def ln_rstd(n, ks):
                dve.wait_ge(dve_var, n)
                newton(rstd[:, ks], nwt[:, ks], mv[:, ks, :, 1], act_rs, n)
                V.scalar_tensor_tensor(nmr[:, ks], mv[:, ks, :, 0], -1.0, rstd[:, ks], ALU.mult, ALU.mult)\
                    .then_inc(dve_rstd, 1)

            def x_tile(b):
                return lambda t: xhat2[:, bass.ds(b * T + t, 1), :].rearrange("p o d -> p (o d)")

            def low(c, b, u):
                dve.wait_ge(act_zhi, z_no(c, b, u) + 1)
                q = slice(u * QT, (u + 1) * QT)
                V.tensor_tensor(zp[c][:, q, H:2 * H], TR[:, 2 if u == 0 else 0, :].rearrange("p (t d) -> p t d", t=QT),
                                zp[c][:, q, 0:H].bitcast(f32), ALU.subtract).then_inc(dve_zlo, 1)

            def convolved(c, i, p, parity, between=None):
                idx, r, q = pair_no(c, i, p), p % 2, slice(2 * p, 2 * p + 2)
                dve.wait_ge(act_aghi, idx + 1)
                ag = AG[:, 2 * r:2 * r + 2, :]
                if c == 0:
                    n = link(V.tensor_scalar_max(deg[:, q], ag[:, :, 2 * H:2 * H + 1], 1.0))
                m = link(V.tensor_tensor(sm[:, r], ag[:, :, H:2 * H], hs[:, r, :, :], ALU.add))
                if c == 0:
                    me.wait(n)
                    m = link(V.reciprocal(rdeg[parity][:, q], deg[:, q]))
                if between is not None:
                    between()
                wait(dve, act_e, idx - 1)
                me.wait(m)
                for j in range(2):
                    m = V.scalar_tensor_tensor(vv[:, r, j, :], sm[:, r, j, :], rdeg[parity][:, 2 * p + j, :],
                                               ag[:, j, 260:260 + H], ALU.mult, ALU.add)
                m.then_inc(dve_v, 1)

            def elu1(i, p):
                r = p % 2
                dve.wait_ge(act_e, pair_no(0, i, p) + 1)
                wait(dve, pe_hT, i * 2)
                V.scalar_tensor_tensor(h1[:, 2 * p:2 * p + 2, :], ee[:, r, :, :], 1.0, vv[:, r, :, :],
                                       ALU.min, ALU.max).then_inc(dve_h, 1)

            def elu2(i, p):
                r = p % 2
                dve.wait_ge(act_e, pair_no(1, i, p) + 1)
                n = link(V.scalar_tensor_tensor(mm_[:, r], ee[:, r, :, :], 1.0, vv[:, r, :, :], ALU.min, ALU.max))
                wait(dve, act_xh2, (i - 1) * T)
                me.wait(n)
                V.scalar_tensor_tensor(x1b[:, 2 * p:2 * p + 2, :], mm_[:, r], -1.0,
                                       xhat2[:, bass.ds((i - 1) * T + 2 * p, 2), :], ALU.add, ALU.add)\
                    .then_inc(dve_h, 1)

            def stats2(i, p):
                dve.wait_ge(dve_h, pair_no(1, i, p) + 1)
                ln_stats(1, lambda t: x1b[:, t, :], (2 * p, 2 * p + 1))

            def keep_stats(b):
                link(V.scalar_tensor_tensor(std2[:, bass.ds(b * T, T)], mv[:, 1, :, 1], EPS, rstd[:, 1],
                                            ALU.add, ALU.mult))
                link(V.tensor_copy(mean2[:, bass.ds(b * T, T)], mv[:, 1, :, 0]))

            def make_mask(b, p, parity):
                dve.wait_ge(adj_in[p % 2], b * 32 + (p // 2 + 1) * 16)
                if not (isinstance(b, int) and b < 2):
                    dve.wait_ge(pe_ag, pair_no(1, b - 1, p) + 1)
                V.tensor_scalar(mask[parity][:, 2 * p, :, :], adj_st[:, p % 2, :, 0:P], 1, None,
                                ALU.is_equal).then_inc(dve_mask, 1)

            def choose(b):
                dve.wait_ge(pe_gate, b + 1)
                link(V.tensor_tensor(logit[:], GP[:, 0:T * E].rearrange("p (t e) -> p t e", e=E),
                                     gate_b[:].unsqueeze(1).broadcast_to([P, T, E]), ALU.add))
                settled()
                for t in range(T):
                    link(V.max(top[:, t, :], logit[:, t, :]))
                settled()
                for t in range(T):
                    link(V.max_index(topi[:, t, :], top[:, t, :], logit[:, t, :]))
                link(V.tensor_copy(gates[:, bass.ds(b * T, T), :], top[:, :, 0:KSEL]))

            def choose_onehot(b):
                me.wait()
                link(V.tensor_copy(sel_e[:].rearrange("p k t -> p t k"), topi[:, :, 0:KSEL]))
                me.wait()
                oh = m12[:, bass.ds(b, 1), :, :, :].rearrange("p o k t e -> p (o k t) e")
                link(V.tensor_tensor(
                    oh, iota_e[:].unsqueeze(1).broadcast_to([P, KSEL * T, E]),
                    sel_e[:].rearrange("p k t -> p (k t)").unsqueeze(2).broadcast_to([P, KSEL * T, E]),
                    ALU.is_equal))
                me.wait()
                oh4 = m12[:, bass.ds(b, 1), :, :, :].rearrange("p o k t e -> p (o k) (t e)")
                V.tensor_tensor(m1[:].rearrange("p t e -> p (t e)"), oh4[:, 0, :], oh4[:, 1, :],
                                ALU.add).then_inc(dve_m1, 1)

            def take_ranks(b):
                dve.wait_ge(pe_rank, b + 1)
                oh = m12[:, bass.ds(b, 1), :, :, :].rearrange("p o k t e -> p (o k) (t e)")
                V.tensor_tensor(rsel[:].rearrange("p k t e -> p k (t e)"), oh,
                                GP[:, T * E:2 * T * E].unsqueeze(1).broadcast_to([P, KSEL, T * E]),
                                ALU.mult).then_inc(dve_rank, 1)
                dve.wait_ge(dve_m1, b + 1)
                link(V.tensor_reduce(msum[:], m1[:].rearrange("p t e -> p e t"), AX.X, ALU.add))
                dve.wait_ge(dve_rank, b + 1)
                link(V.tensor_reduce(rank[:, bass.ds(b, 1), :, :].rearrange("p o k t -> p (o k t)"),
                                     rsel[:].rearrange("p k t e -> p (k t) e"), AX.X, ALU.add))
                me.wait()
                link(V.tensor_tensor(carryf[:], carryf[:], msum[:], ALU.add))
                me.wait()
                V.tensor_copy(carry[:], carryf[:]).then_inc(dve_carry, 1)

            def place_counts(g):
                dve.wait_ge(pe_cnt, g + 1)
                V.tensor_scalar(cnti[:], GP[:, 2 * T * E:2 * T * E + E], float(P - 1), None, ALU.add)\
                    .then_inc(dve_cnt, 1)
                link(V.memset(carryf[:], 0.0))
                dve.wait_ge(dve_cnt, g + 1)
                link(V.tensor_single_scalar(cntt[:], cnti[:], 7, ALU.logical_shift_right))
                me.wait()
                link(V.tensor_copy(ntl[:], cntt[:]))
                V.memset(carry[:], 0.0).then_inc(dve_reset, 1)
                me.wait()
                link(V.tensor_tensor_scan(incl[:], ntl[:], zer16[:], 0.0, ALU.add, ALU.add))
                me.wait()
                link(V.tensor_tensor(base[:], incl[:], ntl[:], ALU.subtract))
                me.wait()
                link(V.tensor_scalar(base[:], base[:], float(P), None, ALU.mult))

            def place_tiles(g):
                n = NO[g] * OCT
                link(V.tensor_tensor(past[:, 0:n], iota_s[:, 0:n].unsqueeze(2).broadcast_to([1, n, E]),
                                     incl[0:1, :].unsqueeze(1).broadcast_to([1, n, E]), ALU.is_ge))
                me.wait()
                link(V.tensor_reduce(emf[:, 0:n], past[:, 0:n], AX.X, ALU.add))
                me.wait()
                link(V.tensor_scalar(emap[0:1, O0[g] * OCT:O0[g + 1] * OCT], emf[:, 0:n], float(E - 1), None,
                                     ALU.min))

            def place(b):
                me.wait()
                link(V.tensor_tensor(rsel[:].rearrange("p k t e -> p (k t) e"),
                                     m12[:, b, :, :, :].rearrange("p k t e -> p (k t) e"),
                                     base[:].unsqueeze(1).broadcast_to([P, KSEL * T, E]), ALU.mult))
                me.wait()
                red = sel_e[:].rearrange("p k t -> p (k t)")
                link(V.tensor_reduce(red, rsel[:].rearrange("p k t e -> p (k t) e"), AX.X, ALU.add))
                me.wait()
                V.tensor_tensor(pos[:, b, :, :].rearrange("p k t -> p (k t)"), red,
                                rank[:, b, :, :].rearrange("p k t -> p (k t)"), ALU.add).then_inc(dve_pos, 1)

            def softmax():
                V.tensor_tensor(gq[:], gates[:, :, 1], gates[:, :, 0], ALU.subtract).then_inc(dve_gd, 1)
                dve.wait_ge(act_gp, 1)
                link(V.tensor_scalar(gq[:], gp[:], 1.0, None, ALU.add))
                me.wait()
                link(V.reciprocal(gates[:, :, 0], gq[:]))
                me.wait()
                link(V.tensor_tensor(gates[:, :, 1], gates[:, :, 0], gp[:], ALU.mult))

            def step(i, parity):
                at = i if isinstance(i, int) else 3
                placing = at == B0[1] + 3
                conv1, conv2, more = at < NB, at > 0, at < NB - 1
                if placing:
                    place_counts(0)
                    place(0)
                if conv1 and conv2:
                    make_mask(i, PAIRS - 1, parity)
                if more:
                    dve.wait_ge(x_in, (i + 2) * 16)
                    dve.sem_inc(passed, 1)
                    ln_stats(0, x_tile(i + 1))
                if not conv1:
                    for u in range(2):
                        low(1, i - 1, u)
                ln_var(kinds(at))
                if conv1:
                    convolved(0, i, 0, parity)
                ln_rstd(i + 2, kinds(at))
                for p in range(1, PAIRS):
                    if conv1:
                        convolved(0, i, p, parity, lambda: elu1(i, p - 1))
                    if conv1 and conv2 and p < 3:
                        low(1, i - 1, p - 1)
                    if p == 2 and at > 1:
                        keep_stats(i - 2)
                    if placing:
                        place(p)
                if at > 2:
                    choose(i - 3)
                last_elu1 = lambda: elu1(i, 3) if conv1 else None
                if not conv2:
                    last_elu1()
                for p in range(PAIRS):
                    if conv2:
                        convolved(1, i, p, 1 - parity, (lambda: elu2(i, p - 1)) if p else last_elu1)
                        if p:
                            stats2(i, p - 1)
                    if p == 0 and at > 2:
                        choose_onehot(i - 3)
                    if p in (1, 2) and more:
                        low(0, i + 1, p - 1)
                    if p < PAIRS - 1 and more:
                        make_mask(i + 1, p, 1 - parity)
                    if p == 2 and at > 2:
                        take_ranks(i - 3)
                if placing:
                    place_tiles(0)
                if conv2:
                    elu2(i, PAIRS - 1)
                    stats2(i, PAIRS - 1)

            dve.wait_ge(x_in, 16)
            ln_stats(0, lambda t: xhat2[:, t, :])
            ln_var(kinds(0))
            ln_rstd(1, kinds(0))
            for p in range(2):
                make_mask(0, p, 0)
            dve.wait_ge(w_in, 16 * N_SMALL)
            dve.wait_ge(act_b1, 1)
            for c in range(2):
                link(V.tensor_tensor(biasf[:, c, :], GP[:, c * H:(c + 1) * H], brow[c][:], ALU.add))
            me.wait()
            link(V.tensor_scalar(biasf[:], biasf[:], 1.0, None, ALU.add))
            me.wait()
            link(V.tensor_copy(bhi[:], biasf[0:2, :, :]))
            me.wait()
            link(V.tensor_tensor(blo[:], biasf[0:2, :, :], bhi[:].bitcast(f32), ALU.subtract))
            dve.wait_ge(pool_const, N_CONST)
            me.wait()
            link(V.tensor_scalar(blo[:], blo[:], ident[0:2, 1:2], None, ALU.mult))
            me.wait()
            V.scalar_tensor_tensor(bhl[:], bhi[:].bitcast(f32), ident[0:2, 0:1], blo[:], ALU.mult, ALU.add)\
                .then_inc(dve_const, 1)
            for u in range(2):
                low(0, 0, u)
            for p in range(2, PAIRS):
                make_mask(0, p, 0)
            for i in range(3):
                step(i, i % 2)
            with dve.Fori(1, (NB - 2) // 2) as k:
                me.enter(k, 1, LINKS_STEPS)
                step(k * 2 + 1, 1)
                step(k * 2 + 2, 0)
            me.leave((NB - 2) // 2 - 1)
            for i in (NB - 1, NB):
                step(i, i % 2)
            ln_var(kinds(NB))
            ln_rstd(NB + 3, kinds(NB))
            place_counts(1)
            keep_stats(NB - 1)
            choose(NB - 2)
            choose_onehot(NB - 2)
            take_ranks(NB - 2)
            for b in range(B0[1], B0[2]):
                place(b)
            place_tiles(1)
            choose(NB - 1)
            choose_onehot(NB - 1)
            take_ranks(NB - 1)
            place_counts(2)

            def copy_weights(s, r, e):
                wait(dve, pe_y, s - (OCT - 1))
                wait(dve, dve_y, s - (OCT - 1))
                V.tensor_copy(wc[:, r % OCT, :], pack[:, bass.ds(e, 1), :].rearrange("p o c -> p (o c)"))\
                    .then_inc(dve_wc, 1)

            def result(s, r):
                u = r // QT
                dve.wait_ge(pe_y, s + 1)
                V.tensor_tensor(ysb[:, u, r % QT, :], YB[r % 2][:, 0:H], wc[:, r, B2C:B2C + H],
                                ALU.add).then_inc(dve_y, 1)

            def experts_of(s):
                return nc.values_load_multi_w_load_instructions(
                    emap[0:1, bass.ds(s, OCT)], engines=(mybir.EngineType.DVE,), min_val=0, max_val=E - 1,
                    skip_runtime_bounds_check_because="place() clamps them to 0..E-1")[1]

            def combine(c, u, part):
                if part == 1:
                    dve.wait_ge(act_gated, c + 1)
                    wait(dve, dve_out, c)
                    y2 = gath[:, u, :, :].rearrange("p (t k) d -> p t k d", k=KSEL)
                    link(V.tensor_tensor(yc, xhat2[:, bass.ds(c * QT, QT), :], y2[:, :, 0, :], ALU.add))
                    me.wait()
                    V.tensor_tensor(yc, yc, y2[:, :, 1, :], ALU.add).then_inc(dve_gath, 1)
                if part == 2:
                    dve.wait_ge(dve_gath, c + 1)
                    dve.sem_inc(passed, 1)
                    for t in range(QT):
                        link(V.bn_stats(stc[:, t, :], yc[:, t, :]))
                if part == 3:
                    settled()
                    for t in range(QT):
                        m = V.bn_aggr(mvc[:, t, :], stc[:, t, :])
                        if t < QT - 1:
                            link(m)
                    m.then_inc(dve_varc, 1)
                if part == 4:
                    dve.wait_ge(act_x1c, (c + 1) * QT)
                    link(V.tensor_tensor(uc, uc, beta[:].unsqueeze(1).broadcast_to([P, QT, H]), ALU.add))
                if part == 5:
                    dve.wait_ge(dve_varc, c + 1)
                    newton(rc0[:], rc1[:], mvc[:, :, 1], act_rsc, c + 1)
                    V.scalar_tensor_tensor(nmc[:], mvc[:, :, 0], -1.0, rc0[:], ALU.mult, ALU.mult)\
                        .then_inc(dve_rstdc, 1)
                if part == 6:
                    dve.wait_ge(dve_rstdc, c + 1)
                    for t in range(ACT_NORMS, QT):
                        link(V.tensor_scalar(yc[:, t, :], yc[:, t, :], rc0[:, t:t + 1], nmc[:, t:t + 1],
                                             ALU.mult, ALU.add))
                if part == 7:
                    dve.wait_ge(act_nc, c + 1)
                    me.wait()
                    link(V.tensor_tensor(yc, yc, gamma[:].unsqueeze(1).broadcast_to([P, QT, H]), ALU.mult))
                    me.wait()
                    wait(dve, o_out[u], (c - u) * 8)
                    V.tensor_tensor(oc[:, u, :, :], yc, uc, ALU.add).then_inc(dve_out, 1)

            def oct(o, first=False, quad=None, placing=False):
                ex = experts_of(o * OCT + AHEAD)
                for r in range(OCT):
                    s = o * OCT + r
                    copy_weights(s + AHEAD, r + AHEAD, ex[r])
                    if not (first and r < LAG):
                        if r % QT == LAG:
                            wait(dve, y_out[r // QT], o * 16)
                        result(s - LAG, (r - LAG) % OCT)
                    if placing and r < GROUPS[2]:
                        place(B0[2] + r)
                    if placing and r == OCT // 2:
                        place_tiles(2)
                    if quad is not None:
                        combine(*quad, r)

            ex = experts_of(0)
            dve.wait_ge(act_pack, 1)
            for r in range(AHEAD):
                copy_weights(r, r, ex[r])
            oct(0, first=True, placing=True)
            softmax()
            with dve.Fori(1, C0) as o:
                oct(o)
            for u in range(2):
                oct(C0 + u, quad=(u, u))
            with dve.Fori(C0 // 2 + 1, O0[NG] // 2) as h:
                me.enter(h, C0 // 2 + 1, 2 * LINKS_COMBINE)
                for u in range(2):
                    oct(h * 2 + u, quad=(h * 2 + (u - C0), u))
            me.leave(O0[NG] // 2 - C0 // 2 - 1)
            for r in range(OCT - LAG, OCT):
                result((O0[NG] - 1) * OCT + r, r)
            with dve.Fori(CT // 2, CQ // 2) as c2:
                me.enter(c2, CT // 2, 2 * LINKS_COMBINE)
                for u in range(2):
                    for part in range(OCT):
                        combine(c2 * 2 + u, u, part)
            me.leave((CQ - CT) // 2)


_INS = ["x", "adj", "L0_gnn_w_rel1", "L0_gnn_w_root1", "L0_gnn_b1", "L0_gnn_w_rel2", "L0_gnn_w_root2",
        "L0_gnn_b2", "L0_ffn_gate_w", "L0_ffn_gate_b", "L0_ffn_w1", "L0_ffn_b1", "L0_ffn_w2", "L0_ffn_b2",
        "L0_ffn_gamma", "L0_ffn_beta"]
_OUTS = [((8, 1024, 128), "float32")]


def kernel(**inputs):
    import numpy as _np
    import concourse.bacc as _bacc
    from concourse import mybir as _mybir
    from concourse.bass_utils import run_bass_kernel_spmd as _run

    nc = _bacc.Bacc("TRN2", target_bir_lowering=False, num_devices=1)
    arrays, args = {}, []
    for name in _INS:
        a = _np.ascontiguousarray(inputs[name])
        arrays[f"in_{name}"] = a
        args.append(nc.dram_tensor(f"in_{name}", a.shape, _mybir.dt.from_np(a.dtype), kind="ExternalInput").ap())
    for i, (shape, dtype) in enumerate(_OUTS):
        dt = _mybir.dt.from_np(_np.dtype(dtype))
        args.append(nc.dram_tensor(f"out_{i}", shape, dt, kind="ExternalOutput").ap())
    gnn_moe_kernel(nc, *args)
    r = _run(nc, [arrays], core_ids=[0])
    return r.results[0]["out_0"]
```
